# Optimizing a Trainium2 kernel written in Bass

```python
import numpy as np
import jax
import jax.numpy as jnp

def _softmax(x, axis=-1):
    return jax.nn.softmax(x, axis=axis)

def _gelu(x):
    return jax.nn.gelu(x, approximate=True)

def _silu(x):
    return jax.nn.silu(x)

def _sigmoid(x):
    return jax.nn.sigmoid(x)

def _layernorm(x, axis=-1, eps=1e-05):
    m = jnp.mean(x, axis=axis, keepdims=True)
    v = jnp.var(x, axis=axis, keepdims=True)
    return (x - m) / jnp.sqrt(v + eps)

def _scatter_add(tgt, idx, src, axis=0):
    return tgt.at[idx].add(src)

def _segment_sum(src, seg, n):
    return jax.ops.segment_sum(src, seg, n)
kernel_name = 'mk_adj_preln_d2_adj_r2_ce2e62'

def setup_inputs(seed: int=0):
    np.random.seed(seed)
    _w = jnp.asarray

    def _rec_inputs():
        import jax
        import jax.numpy as jnp
        _gk = jax.random.key(seed)
        x = -0.0005207 + 1.001 * jax.random.normal(jax.random.fold_in(_gk, 1), (4096, 128), jnp.float32)
        _w = (1.0 + jnp.arange(4096, dtype=jnp.float32)) ** (-0.5)
        _w = _w / _w.mean()
        _pij = jnp.clip(0.00195312 * _w[:, None] * _w[None, :], 0.0, 1.0)
        _a = jax.random.uniform(jax.random.fold_in(_gk, 2), (4096, 4096)) < _pij
        _a = jnp.logical_or(_a, jnp.eye(4096, dtype=bool))
        _af = _a.astype(jnp.float32)
        _af = _af * jax.random.uniform(jax.random.fold_in(_gk, 3), (4096, 4096), jnp.float32, 0.05, 1)
        adj = _af
        return (x, adj)
    x, adj = _rec_inputs()

    def _L0_gnn_setup():
        import jax, jax.numpy as jnp
        import numpy as np
        N = 8192
        IN_DIM = 128
        OUT_DIM = 128

        def _message(X, A, W):
            deg = jnp.sum(A, axis=1, keepdims=True)
            A_norm = A / jnp.where(deg > 0, deg, 1.0)
            return A_norm @ X @ W
        key = jax.random.key(seed)
        k1, k2, k3, k4 = jax.random.split(key, 4)
        X = jax.random.normal(k1, (N, IN_DIM), dtype=jnp.float32)
        A = jax.random.uniform(k2, (N, N), dtype=jnp.float32)
        W_in = jax.random.normal(k3, (IN_DIM, OUT_DIM), dtype=jnp.float32) / np.sqrt(IN_DIM)
        W_out = jax.random.normal(k4, (IN_DIM, OUT_DIM), dtype=jnp.float32) / np.sqrt(IN_DIM)
        return {'X': X, 'A': A, 'W_in': W_in, 'W_out': W_out}
    _L0_gnn_all = _L0_gnn_setup()
    _L0_gnn_in = {k: v for k, v in _L0_gnn_all.items() if k in ('W_in', 'W_out')}
    del _L0_gnn_all

    def _L1_gnn_setup():
        import jax, jax.numpy as jnp
        import numpy as np
        N = 8192
        U = 128
        AVG_DEGREE = 32
        key = jax.random.key(seed)
        kx, ka, kw = jax.random.split(key, 3)
        x = jax.random.normal(kx, (N, U), dtype=jnp.float32)
        adj = (jax.random.uniform(ka, (N, N)) < AVG_DEGREE / N).astype(jnp.float32)
        W = jax.random.normal(kw, (U, U), dtype=jnp.float32) * 0.05
        b = jnp.zeros((U,), dtype=jnp.float32)
        return {'x': x, 'adj': adj, 'W': W, 'b': b}
    _L1_gnn_all = _L1_gnn_setup()
    _L1_gnn_in = {k: v for k, v in _L1_gnn_all.items() if k in ('W', 'b')}
    del _L1_gnn_all
    return {'x': x, 'adj': adj, 'L0_gnn_W_in': _L0_gnn_in['W_in'], 'L0_gnn_W_out': _L0_gnn_in['W_out'], 'L1_gnn_W': _L1_gnn_in['W'], 'L1_gnn_b': _L1_gnn_in['b']}

def reference(x, adj, L0_gnn_W_in, L0_gnn_W_out, L1_gnn_W, L1_gnn_b):
    import jax
    import jax.numpy as jnp

    def _L0_gnn_ref(X, A, W_in, W_out):
        import jax, jax.numpy as jnp
        import numpy as np
        N = 8192
        IN_DIM = 128
        OUT_DIM = 128

        def _message(X, A, W):
            deg = jnp.sum(A, axis=1, keepdims=True)
            A_norm = A / jnp.where(deg > 0, deg, 1.0)
            return A_norm @ X @ W
        X_in = _message(X, A, W_in)
        X_out = _message(X, A.T, W_out)
        return X_in + X_out

    def _L1_gnn_ref(x, adj, W, b):
        import jax, jax.numpy as jnp
        import numpy as np
        N = 8192
        U = 128
        AVG_DEGREE = 32
        adj = jax.lax.stop_gradient(adj)
        neigh1 = adj @ x
        x1 = jax.nn.swish(neigh1 @ W + b)
        neigh2 = adj @ x1
        x2 = jax.nn.swish(neigh2 @ W + b)
        return x2
    h = jnp.maximum(_layernorm(x, axis=-1), 0.0)
    x = x + _L0_gnn_ref(h, adj, L0_gnn_W_in, L0_gnn_W_out)
    h = jnp.maximum(_layernorm(x, axis=-1), 0.0)
    x = x + _L1_gnn_ref(h, adj, L1_gnn_W, L1_gnn_b)
    return x

_drawn_inputs = setup_inputs


def setup_inputs(seed=0):
    import zlib

    import numpy as np

    out = dict(_drawn_inputs(seed))
    spreads = {'L1_gnn_b': (0.0, 0.1)}
    factors = {}
    for name, (base, spread) in spreads.items():
        noise = np.random.default_rng([zlib.crc32(name.encode()), seed]).standard_normal(out[name].shape)
        drawn = base * np.exp(spread * noise) if base else spread * noise
        out[name] = jnp.asarray(drawn.astype(out[name].dtype))
    for name, factor in factors.items():
        out[name] = (out[name] * factor).astype(out[name].dtype)
    return out
```

```python
from contextlib import ExitStack

import concourse.bass as bass
from concourse import mybir

F32, F32R = mybir.dt.float32, mybir.dt.float32r
ACT = mybir.ActivationFunctionType
ALU = mybir.AluOpType
AX = mybir.AxisListType

N = 4096
D = 128
P = 128
NQ, R = 4, 32
SPAN = 1024
HALF = 512
ITERS = N // SPAN
NCX = SPAN // P
C = N // P
STRIPS = HALF // R
QCOLS = SPAN // NQ
PIECES = 2 * C // NCX
UPP = 4
UNITS = PIECES * UPP
PASS_UNITS = ITERS * UNITS
SLOTS = 4
TDEPTH = 4
LEAD = 1
LOAD = 16 * NQ
EPS = 1e-5


def natural_blocks(u):
    return () if u < 2 else (2 * u - 4, 2 * u - 3) if u < 4 else (u,)


def gnn_kernel(nc, x, adj, w_in, w_out, w_sage, bias, out):
    ctx = ExitStack()
    with ctx:
        def sb(name, shape, dt=F32):
            return ctx.enter_context(nc.sbuf_tensor(name, shape, dt))

        def bank(name):
            return ctx.enter_context(nc.psum_tensor(name, [P, HALF], F32))

        def sem(name):
            return ctx.enter_context(nc.semaphore(name))

        raw = sb("raw", [P, SLOTS, STRIPS * QCOLS])
        turned = sb("turned", [P, TDEPTH, 2, HALF])
        high = sb("high", [P, 4, HALF], F32R)
        low = sb("low", [P, 4, HALF], F32R)
        h_full = sb("h_full", [P, C, D])
        h_high = sb("h_high", [P, C, D], F32R)
        h_low = sb("h_low", [P, C, D], F32R)
        y_full = sb("y_full", [P, C // 2, D])
        y_high = sb("y_high", [P, C // 2, D], F32R)
        y_low = sb("y_low", [P, C // 2, D], F32R)
        x2 = sb("x2", [P, C, D])
        p2 = sb("p2", [P, C, D])
        w_in_sb = sb("w_in_sb", [P, D])
        w_out_sb = sb("w_out_sb", [P, D])
        w_sage_sb = sb("w_sage_sb", [P, D])
        bias_row = sb("bias_row", [1, 4, D])
        ones_row = sb("ones_row", [1, P])
        row_part = sb("row_part", [P, ITERS * C])
        col_part = sb("col_part", [P, 2 * ITERS * C])
        stats = sb("stats", [P, NCX, 6])
        mean_var = sb("mean_var", [P, NCX, 2])
        spread = sb("spread", [P, 2, NCX])
        deg = sb("deg", [P, 2, C])
        positive = sb("positive", [P, 2, C])
        inv_deg = sb("inv_deg", [P, 2, C])

        stage = y_full[:, :, :].rearrange("p (z c q) (t s) -> p z c (q t) s", z=2, c=NCX, t=4)
        discard = y_low[:, 0:NCX, :].rearrange("p c d -> p (c d)")
        x_rows = raw[:, SLOTS - 1, :].rearrange("p (c d) -> p c d", d=D)
        small = p2[:, :, :].rearrange("p (z b) d -> p z (b d)", b=4)
        late_stage = small[:, 2:4, :].rearrange("p z x -> p (z x)").rearrange(
            "p (c q s) -> p c q s", c=NCX, q=NQ)

        half_sum = [bank("half_sum0"), bank("half_sum1")]
        panel_sum = [bank("panel_sum0"), bank("panel_sum1")]
        project = [bank("project0"), bank("project1")]

        x_in = sem("x_in")
        w_loaded = sem("w_loaded")
        ones_set = sem("ones_set")
        slot_in = [sem(f"slot_in{i}") for i in range(SLOTS)]
        unit_turned = sem("unit_turned")
        high_ready = sem("high_ready")
        low_ready = sem("low_ready")
        pool_low_ready = sem("pool_low_ready")
        unit_used = sem("unit_used")
        natural_used = sem("natural_used")
        row_summed = sem("row_summed")
        half_staged = sem("half_staged")
        panel_staged = sem("panel_staged")
        project_done = sem("project_done")
        project_read = sem("project_read")
        dve_step = sem("dve_step")
        var_ready = sem("var_ready")
        std_ready = sem("std_ready")
        h_written = sem("h_written")
        h_high_ready = sem("h_high_ready")
        h_ready = sem("h_ready")
        x_used = sem("x_used")
        y_high_ready = sem("y_high_ready")
        y_ready = sem("y_ready")
        swish_ready = sem("swish_ready")
        sum_ready = sem("sum_ready")
        stored = sem("stored")

        block = ctx.enter_context(nc.Block())

        def turned_slot(unit):
            return unit % TDEPTH

        def split_free(ps, u, unit):
            if ps == 0:
                return unit - 1
            if ps == 1 and isinstance(unit, int) and u < 4:
                return PASS_UNITS - 1 if u < 2 else PASS_UNITS
            return unit - 3

        def wait_unless_none(eng, sem_, value):
            if not isinstance(value, int) or value > 0:
                eng.wait_ge(sem_, value)

        @block.sync
        def _(sp):
            def load_turned(e, v, slot):
                h, k = divmod(e, C // NCX)
                for q in range(NQ):
                    src = adj[bass.ds(v * SPAN + h * HALF, HALF), SPAN * k + QCOLS * q:SPAN * k + QCOLS * (q + 1)]
                    sp.dma_start(raw[R * q:R * (q + 1), slot, :].rearrange("p (g x) -> p g x", g=STRIPS),
                                 src.rearrange("(g s) x -> s g x", s=R)).then_inc(slot_in[slot], 16)

            def load_natural(e, v, slot):
                k, hh = divmod(e, 2)
                for q in (1, 2, 3, 0):
                    r0 = SPAN * k + QCOLS * q + P * hh
                    src = adj[r0:r0 + P, bass.ds(v * SPAN, SPAN)]
                    sp.dma_start(raw[R * q:R * (q + 1), slot, :].rearrange("p (j x) -> p j x", j=4),
                                 src.rearrange("(j r) x -> r j x", r=R)).then_inc(slot_in[slot], 16)

            def load_x():
                for k in range(C // NCX):
                    for q in range(NQ):
                        r0 = SPAN * k + QCOLS * q
                        sp.dma_start(x_rows[R * q:R * (q + 1), NCX * k:NCX * (k + 1), :],
                                     x[r0:r0 + QCOLS, :].rearrange("(c r) d -> r c d", r=R)).then_inc(x_in, 16)

            def pass0(v):
                for e in range(PIECES):
                    n = v * PIECES + e
                    if not isinstance(n, int) or n >= 2:
                        sp.wait_ge(unit_turned, (n - 1) * UPP)
                    load_turned(e, v, 2 * (e % 2))
                    if not isinstance(n, int) or n >= 2:
                        sp.wait_ge(natural_used, n - 1)
                        sp.wait_ge(row_summed, (n - 1) * 4)
                    elif n == 1:
                        sp.wait_ge(h_written, ITERS)
                    load_natural(e, v, 2 * (e % 2) + 1)

            def store(v, g):
                sp.wait_ge(sum_ready, v * 2 + g + 1)
                for q in range(NQ):
                    sp.dma_start(out[bass.ds(v * SPAN + QCOLS * q + P * g, P), :].rearrange("(j r) d -> r j d", r=R),
                                 x2[R * q:R * (q + 1), bass.ds(v * NCX + 4 * g, 4), :]).then_inc(stored, 16)

            def later_pass(ps, v, stores):
                for e in range(PIECES):
                    if ps == 1 and isinstance(v, int) and v == 0 and e < SLOTS:
                        if e % 2 == 0:
                            sp.wait_ge(unit_turned, PASS_UNITS - (1 - e // 2) * UPP)
                        elif e == 1:
                            sp.wait_ge(natural_used, ITERS * PIECES - 1)
                            sp.wait_ge(row_summed, ITERS * C - 4)
                            load_turned(e, v, e)
                            sp.wait_ge(natural_used, ITERS * PIECES)
                            sp.wait_ge(row_summed, ITERS * C)
                            load_x()
                            continue
                        else:
                            sp.wait_ge(x_used, C)
                    else:
                        sp.wait_ge(unit_turned, ps * PASS_UNITS + v * UNITS + (e - 3) * UPP)
                    load_turned(e, v, e % SLOTS)
                    if stores and e == 3:
                        store(v - 1, 0)
                        store(v - 1, 1)

            load_x()
            for dst, src in ((w_in_sb, w_in), (w_out_sb, w_out), (w_sage_sb, w_sage)):
                sp.dma_start(dst[:, :], src).then_inc(w_loaded, 16)
            for j in range(4):
                sp.dma_start(bias_row[0:1, j, :], bias.rearrange("(a d) -> a d", a=1)).then_inc(w_loaded, 16)
            pass0(0)
            with sp.Fori(1, ITERS) as v:
                pass0(v)
            for ps in (1, 2):
                later_pass(ps, 0, False)
                with sp.Fori(1, ITERS) as v:
                    later_pass(ps, v, ps == 2)
            store(ITERS - 1, 0)
            store(ITERS - 1, 1)
            sp.wait_ge(stored, 2 * ITERS * LOAD)

        @block.vector
        def _(dve):
            steps = [0]

            def step(ins):
                steps[0] += 1
                ins.then_inc(dve_step, 1)

            def settle():
                dve.wait_ge(dve_step, steps[0])

            def turn(ps, v, u):
                unit = ps * PASS_UNITS + v * UNITS + u
                e, w = divmod(u, UPP)
                if ps == 0:
                    slot, loads = 2 * (e % 2), v * (PIECES // 2) + e // 2 + 1
                else:
                    slot = e % SLOTS
                    loads = ITERS * PIECES // 2 + ((ps - 1) * ITERS + v) * (PIECES // SLOTS) + e // SLOTS + 1
                if w == 0:
                    dve.wait_ge(slot_in[slot], loads * LOAD)
                wait_unless_none(dve, unit_used, unit - TDEPTH + 1)
                src = raw[:, slot, :].rearrange("p (g x) -> p g x", g=STRIPS)[:, :, 64 * w:64 * (w + 1)]
                dst = turned[:, turned_slot(u), :, :].rearrange("p c (g s) -> p g c s", s=R)
                nc.vector.transpose(dst, src).then_inc(unit_turned, 1)

            def split_low(ps, v, u):
                unit = ps * PASS_UNITS + v * UNITS + u
                dve.wait_ge(high_ready, unit + 1)
                wait_unless_none(dve, unit_used, split_free(ps, u, unit))
                t = turned[:, turned_slot(u), :, :]
                if ps == 0:
                    s = 2 * (u % 2)
                    nc.vector.tensor_tensor(low[:, s:s + 2, :], t, high[:, s:s + 2, :].bitcast(F32),
                                            ALU.subtract).then_inc(low_ready, 1)
                else:
                    nc.vector.tensor_tensor(low[:, u % 4, :], t[:, 1, :], high[:, u % 4, :].bitcast(F32),
                                            ALU.subtract).then_inc(low_ready, 1)

            def stage_half(v, h):
                dve.wait_ge(unit_used, v * UNITS + (h + 1) * (UNITS // 2))
                if h == 0:
                    wait_unless_none(dve, project_done, v * 4)
                nc.vector.tensor_copy(stage[:, 0, :, 2 * h:2 * h + 2, :].rearrange("p c q s -> p q c s"),
                                      half_sum[h][:, :].rearrange("p (q c s) -> p q c s", q=2, s=R)
                                      ).then_inc(half_staged, 1)

            def stage_panel(v):
                dve.wait_ge(natural_used, (v + 1) * PIECES)
                for h in range(2):
                    last = nc.vector.tensor_copy(stage[:, 1, :, 2 * h:2 * h + 2, :].rearrange("p c q s -> p q c s"),
                                                 panel_sum[h][:, :].rearrange("p (q c s) -> p q c s", q=2, s=R))
                    last.then_inc(panel_staged, 1)

            def keep_project(v, g):
                dve.wait_ge(project_done, v * 4 + g + 1)
                dst = (x2 if g < 2 else p2)[:, :, :].rearrange("p c d -> p (c d)")
                nc.vector.tensor_copy(dst[:, bass.ds(v * SPAN + (g % 2) * HALF, HALF)],
                                      project[g % 2][:, :]).then_inc(project_read, 1)

            def pass0(v, prev):
                turn(0, v, 0)
                for u in range(UNITS):
                    if u + 1 < UNITS:
                        turn(0, v, u + 1)
                    split_low(0, v, u)
                    if prev is not None and u == 1:
                        stage_half(prev, 1)
                        stage_panel(prev)
                    if prev is not None and u in (6, 8):
                        for g in (0, 1):
                            keep_project(prev, u - 6 + g)
                    if u == 17:
                        stage_half(v, 0)

            def norm_relu(src, g, call):
                blocks = range(NCX * g, NCX * (g + 1))
                for j, c in enumerate(blocks):
                    step(nc.vector.bn_stats(stats[:, j, :], src[:, c, :]))
                settle()
                for j in range(NCX):
                    step(nc.vector.bn_aggr(mean_var[:, j, :], stats[:, j, :]))
                settle()
                nc.vector.tensor_scalar(spread[:, 0, :], mean_var[:, :, 1], EPS, None, ALU.add).then_inc(var_ready, 1)
                dve.wait_ge(std_ready, call + 1)
                step(nc.vector.reciprocal(spread[:, 0, :], spread[:, 1, :]))
                settle()
                for j, c in enumerate(blocks):
                    step(nc.vector.tensor_scalar(h_full[:, c, :], src[:, c, :], mean_var[:, j, 0:1],
                                                 spread[:, 0, j:j + 1], ALU.subtract, ALU.mult))
                settle()
                group = slice(NCX * g, NCX * (g + 1))
                nc.vector.tensor_scalar(h_full[:, group, :], h_full[:, group, :], 0.0, None,
                                        ALU.max).then_inc(h_written, 1)
                dve.wait_ge(h_written, call + 1)
                dve.wait_ge(h_high_ready, call + 1)
                nc.vector.tensor_tensor(h_low[:, group, :], h_full[:, group, :],
                                        h_high[:, group, :].bitcast(F32), ALU.subtract).then_inc(h_ready, 1)

            nc.vector.memset(ones_row[:, :], 1.0).then_inc(ones_set, 1)
            dve.wait_ge(x_in, 16 * 16)
            for g in range(ITERS):
                norm_relu(x_rows, g, g)

            pass0(0, None)
            with dve.Fori(1, ITERS) as v:
                pass0(v, v - 1)
            last = ITERS - 1
            stage_half(last, 1)
            stage_panel(last)
            for g in range(4):
                keep_project(last, g)

            dve.wait_ge(row_summed, ITERS * C)
            dve.wait_ge(high_ready, PASS_UNITS)
            step(nc.vector.tensor_reduce(deg[:, 0, :], row_part[:, :].rearrange("p (v c) -> p c v", c=C),
                                         AX.X, ALU.add))
            step(nc.vector.tensor_reduce(deg[:, 1, :], col_part[:, :].rearrange("p (v c) -> p c v", c=C),
                                         AX.X, ALU.add))
            settle()
            step(nc.vector.tensor_scalar(positive[:, :, :], deg[:, :, :], 0.0, None, ALU.is_gt))
            settle()
            step(nc.vector.tensor_tensor(deg[:, :, :], deg[:, :, :], positive[:, :, :], ALU.mult))
            settle()
            step(nc.vector.tensor_tensor(deg[:, :, :], deg[:, :, :], positive[:, :, :], ALU.subtract))
            settle()
            step(nc.vector.tensor_scalar(deg[:, :, :], deg[:, :, :], 1.0, None, ALU.add))
            settle()
            step(nc.vector.reciprocal(inv_deg[:, :, :], deg[:, :, :]))
            dve.wait_ge(project_read, 4 * ITERS)
            dve.wait_ge(x_in, 2 * 16 * 16)
            settle()
            for g in range(ITERS):
                for c in range(NCX * g, NCX * (g + 1)):
                    nc.vector.scalar_tensor_tensor(out=x2[:, c, :], in0=x2[:, c, :], scalar=inv_deg[:, 0, c:c + 1],
                                                   in1=x_rows[:, c, :], op0=ALU.mult, op1=ALU.add).then_inc(x_used, 1)
                dve.wait_ge(x_used, NCX * (g + 1))
                for c in range(NCX * g, NCX * (g + 1)):
                    step(nc.vector.scalar_tensor_tensor(out=x2[:, c, :], in0=p2[:, c, :], scalar=inv_deg[:, 1, c:c + 1],
                                                        in1=x2[:, c, :], op0=ALU.mult, op1=ALU.add))
                settle()
                norm_relu(x2, g, ITERS + g)

            def finish_y(v):
                for g in range(2):
                    dve.wait_ge(y_high_ready, v * 2 + g + 1)
                    nc.vector.tensor_tensor(y_low[:, bass.ds(v * 4 + 2 * g, 2), :],
                                            small[:, g, 0:2 * D].rearrange("p (c d) -> p c d", d=D),
                                            y_high[:, bass.ds(v * 4 + 2 * g, 2), :].bitcast(F32),
                                            ALU.subtract).then_inc(y_ready, 1)

            def finish_out(v):
                for g in range(2):
                    dve.wait_ge(swish_ready, v * 2 + g + 1)
                    place = x2[:, bass.ds(v * NCX + 4 * g, 4), :]
                    nc.vector.tensor_tensor(place, small[:, g, :].rearrange("p (c d) -> p c d", d=D), place,
                                            ALU.add).then_inc(sum_ready, 1)

            def later_pass(ps, v, finish):
                turn(ps, v, 0)
                for u in range(UNITS):
                    if u + 1 < UNITS:
                        turn(ps, v, u + 1)
                    if u % 2 == 0:
                        split_low(ps, v, u)
                    if finish is not None and u == 10:
                        finish()

            later_pass(1, 0, None)
            with dve.Fori(1, ITERS) as v:
                later_pass(1, v, lambda: finish_y(v - 1))
            later_pass(2, 0, lambda: finish_y(ITERS - 1))
            with dve.Fori(1, ITERS) as v:
                later_pass(2, v, lambda: finish_out(v - 1))
            finish_out(ITERS - 1)

        @block.gpsimd
        def _(pool):
            def later_pass(ps, v):
                for u in range(1, UNITS, 2):
                    unit = ps * PASS_UNITS + v * UNITS + u
                    pool.wait_ge(high_ready, unit + 1)
                    pool.wait_ge(unit_used, split_free(ps, u, unit))
                    nc.gpsimd.tensor_tensor(low[:, u % 4, :], turned[:, turned_slot(u), 1, :],
                                            high[:, u % 4, :].bitcast(F32), ALU.subtract).then_inc(pool_low_ready, 1)

            for ps in (1, 2):
                later_pass(ps, 0)
                with pool.Fori(1, ITERS) as v:
                    later_pass(ps, v)

        @block.scalar
        def _(act):
            def split_high(ps, v, u):
                unit = ps * PASS_UNITS + v * UNITS + u
                act.wait_ge(unit_turned, unit + 1)
                wait_unless_none(act, unit_used, split_free(ps, u, unit))
                t = turned[:, turned_slot(u), :, :]
                if ps == 0:
                    h, c = divmod(2 * u, C)
                    for j in range(2):
                        ins = nc.scalar.activation(
                            high[:, 2 * (u % 2) + j, :], t[:, j, :], ACT.Copy,
                            accum_out=col_part[:, bass.ds(v * 2 * C + h * C + c + j, 1)])
                    ins.then_inc(high_ready, 1)
                else:
                    nc.scalar.activation(high[:, u % 4, :], t[:, 1, :], ACT.Copy).then_inc(high_ready, 1)

            def sum_rows(v, b):
                e, j = divmod(b, 4)
                slot = 2 * (e % 2) + 1
                if j == 0:
                    act.wait_ge(slot_in[slot], (v * (PIECES // 2) + e // 2 + 1) * LOAD)
                wait_unless_none(act, row_summed, v * C + b)
                nc.scalar.activation(discard, raw[:, slot, SPAN * j:SPAN * (j + 1)], ACT.Copy,
                                     accum_out=row_part[:, bass.ds(v * C + b, 1)]).then_inc(row_summed, 1)

            def norm_help(call):
                g = call % ITERS
                act.wait_ge(var_ready, call + 1)
                nc.scalar.activation(spread[:, 1, :], spread[:, 0, :], ACT.Sqrt).then_inc(std_ready, 1)
                act.wait_ge(h_written, call + 1)
                nc.scalar.activation(h_high[:, NCX * g:NCX * (g + 1), :], h_full[:, NCX * g:NCX * (g + 1), :],
                                     ACT.Copy).then_inc(h_high_ready, 1)

            for call in range(ITERS):
                norm_help(call)

            def pass0(v):
                for u in range(UNITS):
                    split_high(0, v, u)
                    sum_rows(v, u)

            pass0(0)
            with act.Fori(1, ITERS) as v:
                pass0(v)
            for call in range(ITERS, 2 * ITERS):
                norm_help(call)

            def stage_half(ps, v, h):
                act.wait_ge(unit_used, (ps * ITERS + v) * UNITS + (h + 1) * (UNITS // 2))
                act.wait_ge(project_done, 4 * ITERS + ((ps - 1) * ITERS + v) * 2)
                nc.scalar.activation(late_stage[:, :, 2 * h:2 * h + 2, :].rearrange("p c q s -> p q c s"),
                                     half_sum[h][:, :].rearrange("p (q c s) -> p q c s", q=2, s=R),
                                     ACT.Copy).then_inc(half_staged, 1)

            def swish_y(v):
                for g in range(2):
                    act.wait_ge(project_done, 4 * ITERS + v * 2 + g + 1)
                    z = project[g][:, :].rearrange("p (b two d) -> p b two d", two=2, d=D)
                    nc.scalar.activation(y_full[:, bass.ds(v * 4 + 2 * g, 2), :], z[:, :, 0, :], ACT.Silu)
                    nc.scalar.activation(small[:, g, 0:2 * D].rearrange("p (c d) -> p c d", d=D), z[:, :, 1, :],
                                         ACT.Silu)
                    nc.scalar.activation(y_high[:, bass.ds(v * 4 + 2 * g, 2), :], z[:, :, 1, :],
                                         ACT.Silu).then_inc(y_high_ready, 1)

            def swish_out(v):
                for g in range(2):
                    act.wait_ge(project_done, 6 * ITERS + v * 2 + g + 1)
                    act.wait_ge(y_ready, 2 * ITERS)
                    nc.scalar.activation(small[:, g, :], project[g][:, :], ACT.Silu).then_inc(swish_ready, 1)

            def later_pass(ps, v, prev, swish):
                for u in range(UNITS):
                    split_high(ps, v, u)
                    if prev is not None and u == 3:
                        stage_half(prev[0], prev[1], 1)
                    if prev is not None and u == 8:
                        swish()
                    if u == 19:
                        stage_half(ps, v, 0)

            later_pass(1, 0, None, None)
            with act.Fori(1, ITERS) as v:
                later_pass(1, v, (1, v - 1), lambda: swish_y(v - 1))
            later_pass(2, 0, (1, ITERS - 1), lambda: swish_y(ITERS - 1))
            with act.Fori(1, ITERS) as v:
                later_pass(2, v, (2, v - 1), lambda: swish_out(v - 1))
            stage_half(2, ITERS - 1, 1)
            swish_out(ITERS - 1)

        @block.tensor
        def _(pe):
            def turned_unit(ps, v, u):
                unit = ps * PASS_UNITS + v * UNITS + u
                h, c = divmod(2 * u, C)
                if u % (UNITS // 2) == 0:
                    wait_unless_none(pe, half_staged, (ps * ITERS + v) * 2 + h - 1)
                pe.wait_ge(high_ready, unit + 1)
                if ps == 0:
                    pe.wait_ge(low_ready, unit + 1)
                elif u % 2 == 0:
                    pe.wait_ge(low_ready, PASS_UNITS + ((ps - 1) * ITERS + v) * (UNITS // 2) + u // 2 + 1)
                else:
                    pe.wait_ge(pool_low_ready, ((ps - 1) * ITERS + v) * (UNITS // 2) + u // 2 + 1)
                acc = half_sum[h][:, :]
                if ps > 0:
                    whole = h_full[:, c, :] if ps == 1 else y_full[:, c // 2, :]
                    nc.tensor.matmul(acc, whole, turned[:, turned_slot(u), 0, :], start=c == 0, stop=False)
                for j in range(2) if ps == 0 else (1,):
                    s = 2 * (u % 2) + j if ps == 0 else u % 4
                    if ps < 2:
                        hh, hl = h_high[:, c + j, :], h_low[:, c + j, :]
                    else:
                        hh, hl = y_high[:, c // 2, :], y_low[:, c // 2, :]
                    nc.tensor.matmul(acc, hh, high[:, s, :], start=ps == 0 and c + j == 0, stop=False)
                    nc.tensor.matmul(acc, hh, low[:, s, :], start=False, stop=False)
                    ins = nc.tensor.matmul(acc, hl, high[:, s, :], start=False, stop=c + j == C - 1)
                return ins

            def natural(v, b):
                e, j = divmod(b, 4)
                slot = 2 * (e % 2) + 1
                if j == 0:
                    pe.wait_ge(slot_in[slot], (v * (PIECES // 2) + e // 2 + 1) * LOAD)
                if b == 0:
                    wait_unless_none(pe, panel_staged, v * 2)
                for hh in range(2):
                    a = raw[:, slot, SPAN * j + HALF * hh:SPAN * j + HALF * (hh + 1)]
                    ins = nc.tensor.matmul(panel_sum[hh][:, :], h_full[:, b, :], a, start=b == 0, stop=b == C - 1)
                if j == 3:
                    ins.then_inc(natural_used, 1)

            def weights0(v, z):
                pe.wait_ge(half_staged, v * 2 + 2)
                pe.wait_ge(panel_staged, v * 2 + 2)
                for g in range(2):
                    if z == 1:
                        pe.wait_ge(project_read, v * 4 + g + 1)
                    for j in range(4):
                        ins = nc.tensor.matmul(project[g][:, D * j:D * (j + 1)],
                                               stage[:, z, 4 * g + j, :, :].rearrange("p q s -> p (q s)"),
                                               (w_in_sb if z == 0 else w_out_sb)[:, :], start=True, stop=True)
                    ins.then_inc(project_done, 1)

            def later_weights(ps, v):
                pe.wait_ge(half_staged, (ps * ITERS + v) * 2 + 2)
                for g in range(2):
                    pe.wait_ge(*((project_read, 4 * ITERS) if ps == 1 else (y_high_ready, 2 * ITERS)))
                    nc.tensor.matmul(project[g][:, :], ones_row[:, :], bias_row[:, :, :].rearrange("p j d -> p (j d)"),
                                     start=True, stop=False)
                    for j in range(4):
                        ins = nc.tensor.matmul(project[g][:, D * j:D * (j + 1)],
                                               late_stage[:, 4 * g + j, :, :].rearrange("p q s -> p (q s)"),
                                               w_sage_sb[:, :], start=False, stop=j == 3)
                    ins.then_inc(project_done, 1)

            def pass0(v, prev):
                for u in range(UNITS):
                    if u < UNITS // 2 and isinstance(v, int) and u % 4 == 0:
                        pe.wait_ge(h_ready, u // 4 + 1)
                    ins = turned_unit(0, v, u)
                    ins.then_inc(unit_used, 1)
                    for b in natural_blocks(u):
                        natural(v, b)
                    if prev is not None and u in (3, 5):
                        weights0(prev, (u - 3) // 2)

            pe.wait_ge(w_loaded, 7 * 16)
            pe.wait_ge(ones_set, 1)
            pass0(0, None)
            with pe.Fori(1, ITERS) as v:
                pass0(v, v - 1)
            weights0(ITERS - 1, 0)
            weights0(ITERS - 1, 1)

            def later_pass(ps, v, prev):
                for u in range(UNITS):
                    if isinstance(v, int) and ps == 1 and u < UNITS // 2 and u % 4 == 0:
                        pe.wait_ge(h_ready, ITERS + u // 4 + 1)
                    if isinstance(v, int) and ps == 2 and u < UNITS // 2 and u % 4 == 0:
                        pe.wait_ge(y_ready, 2 * (u // 4 + 1))
                    ins = turned_unit(ps, v, u)
                    ins.then_inc(unit_used, 1)
                    if prev is not None and u == 4:
                        later_weights(*prev)

            later_pass(1, 0, None)
            with pe.Fori(1, ITERS) as v:
                later_pass(1, v, (1, v - 1))
            later_pass(2, 0, (1, ITERS - 1))
            with pe.Fori(1, ITERS) as v:
                later_pass(2, v, (2, v - 1))
            later_weights(2, ITERS - 1)


_INS = ["x", "adj", "L0_gnn_W_in", "L0_gnn_W_out", "L1_gnn_W", "L1_gnn_b"]


def kernel(**inputs):
    import numpy as _np
    import concourse.bacc as _bacc
    from concourse import mybir as _mybir
    from concourse.bass_utils import run_bass_kernel_spmd as _run

    nc = _bacc.Bacc("TRN2", target_bir_lowering=False, num_devices=1)
    arrays, args = {}, []
    for name in _INS:
        a = _np.ascontiguousarray(inputs[name])
        arrays[f"in_{name}_dram"] = a
        args.append(nc.dram_tensor(f"in_{name}_dram", a.shape, _mybir.dt.from_np(a.dtype), kind="ExternalInput").ap())
    args.append(nc.dram_tensor("out_0_dram", (4096, 128), _mybir.dt.float32, kind="ExternalOutput").ap())
    gnn_kernel(nc, *args)
    r = _run(nc, [arrays], core_ids=[0])
    return r.results[0]["out_0_dram"]
```

```python
from contextlib import ExitStack

import concourse.bass as bass
from concourse import mybir

F32, F32R = mybir.dt.float32, mybir.dt.float32r
ACT = mybir.ActivationFunctionType
ALU = mybir.AluOpType
AX = mybir.AxisListType

N = 4096
D = 128
P = 128
NQ, R = 4, 32
SPAN = 1024
HALF = 512
ITERS = N // SPAN
NCX = SPAN // P
C = N // P
STRIPS = HALF // R
QCOLS = SPAN // NQ
PIECES = 2 * C // NCX
UPP = 4
UNITS = PIECES * UPP
PASS_UNITS = ITERS * UNITS
SLOTS = 4
TDEPTH = 4
SLOT_OF = (0, 2, 3, 1)
DVE_NORMS = (0, 1, 4)
WHOLE = UNITS // 2
LOAD = 16 * NQ
EPS = 1e-5


def natural_blocks(u):
    return () if u < 2 else (2 * u - 4, 2 * u - 3) if u < 4 else (u,)


def gnn_kernel(nc, x, adj, w_in, w_out, w_sage, bias, out):
    ctx = ExitStack()
    with ctx:
        def sb(name, shape, dt=F32):
            return ctx.enter_context(nc.sbuf_tensor(name, shape, dt))

        def bank(name):
            return ctx.enter_context(nc.psum_tensor(name, [P, HALF], F32))

        def sem(name):
            return ctx.enter_context(nc.semaphore(name))

        raw = sb("raw", [P, SLOTS, STRIPS * QCOLS])
        turned = sb("turned", [P, TDEPTH, 2, HALF])
        high = sb("high", [P, 4, HALF], F32R)
        low = sb("low", [P, 4, HALF], F32R)
        h_full = sb("h_full", [P, C, D])
        h_high = sb("h_high", [P, C, D], F32R)
        h_low = sb("h_low", [P, C, D], F32R)
        y_full = sb("y_full", [P, C // 2, D])
        y_high = sb("y_high", [P, C // 2, D], F32R)
        y_low = sb("y_low", [P, C // 2, D], F32R)
        x2 = sb("x2", [P, C, D])
        p2 = sb("p2", [P, C, D])
        w_in_sb = sb("w_in_sb", [P, D])
        w_out_sb = sb("w_out_sb", [P, D])
        w_sage_sb = sb("w_sage_sb", [P, D])
        bias_row = sb("bias_row", [1, 4, D])
        ones_row = sb("ones_row", [1, P])
        row_part = sb("row_part", [P, ITERS * C])
        col_part = sb("col_part", [P, 2 * ITERS * C])
        stats = sb("stats", [P, NCX, 6])
        mean_var = sb("mean_var", [P, NCX, 2])
        var = sb("var", [P, 2, NCX])
        std = sb("std", [P, 2, NCX])
        inv_std = sb("inv_std", [P, 2, NCX])
        shift = sb("shift", [P, 2, NCX])
        deg = sb("deg", [P, 2, C])
        positive = sb("positive", [P, 2, C])
        inv_deg = sb("inv_deg", [P, 2, C])

        stage = y_full[:, :, :].rearrange("p (z c q) (t s) -> p z c (q t) s", z=2, c=NCX, t=4)
        discard = y_low[:, 0:NCX, :].rearrange("p c d -> p (c d)")
        x_rows = [x2, raw[:, 1, :].rearrange("p (c d) -> p c d", d=D)]
        small = p2[:, :, :].rearrange("p (z b) d -> p z (b d)", b=4)
        late_stage = small[:, 2:4, :].rearrange("p z x -> p (z x)").rearrange(
            "p (c q s) -> p c q s", c=NCX, q=NQ)

        half_sum = [bank("half_sum0"), bank("half_sum1")]
        panel_sum = [bank("panel_sum0"), bank("panel_sum1")]
        project = [bank("project0"), bank("project1")]

        x_in = [sem(f"x_in{k}") for k in range(C // NCX)]
        w_loaded = sem("w_loaded")
        ones_set = sem("ones_set")
        slot_in = [sem(f"slot_in{i}") for i in range(SLOTS)]
        unit_turned = sem("unit_turned")
        high_ready = sem("high_ready")
        low_ready = sem("low_ready")
        pool_low_ready = sem("pool_low_ready")
        unit_used = sem("unit_used")
        natural_used = sem("natural_used")
        row_summed = sem("row_summed")
        half_staged = sem("half_staged")
        panel_staged = sem("panel_staged")
        project_done = sem("project_done")
        project_read = sem("project_read")
        dve_step = sem("dve_step")
        var_ready = sem("var_ready")
        std_ready = sem("std_ready")
        scale_ready = sem("scale_ready")
        h_written = sem("h_written")
        deg_ready = sem("deg_ready")
        x_added = sem("x_added")
        x_scaled = sem("x_scaled")
        h_high_ready = sem("h_high_ready")
        h_ready = sem("h_ready")
        y_high_ready = sem("y_high_ready")
        y_ready = sem("y_ready")
        swish_ready = sem("swish_ready")
        sum_ready = sem("sum_ready")
        stored = sem("stored")

        block = ctx.enter_context(nc.Block())

        def turned_slot(unit):
            return unit % TDEPTH

        def split_free(ps, unit):
            return unit - 1 if ps == 0 else unit - 3

        def splits(ps, v, u):
            before = ps * PASS_UNITS + v * UNITS + u
            return before if ps == 0 or (ps == 1 and isinstance(v, int) and v == 0 and u < WHOLE) else before - WHOLE

        def splits_of_kind(ps, v, u):
            before = ps * (PASS_UNITS // 2) + v * (UNITS // 2) + u // 2
            return before if ps == 0 else before - WHOLE // 2

        def whole_unit(ps, v, u):
            return ps == 1 and isinstance(v, int) and v == 0 and u < WHOLE

        def wait_unless_none(eng, sem_, value):
            if not isinstance(value, int) or value > 0:
                eng.wait_ge(sem_, value)

        def load_x_spans(eng, at, spans):
            for k in spans:
                for q in range(NQ):
                    r0 = SPAN * k + QCOLS * q
                    eng.dma_start(x_rows[at][R * q:R * (q + 1), NCX * k:NCX * (k + 1), :],
                                  x[r0:r0 + QCOLS, :].rearrange("(c r) d -> r c d", r=R)).then_inc(x_in[k], 16)

        @block.sync
        def _(sp):
            def load_turned(e, v, slot):
                h, k = divmod(e, C // NCX)
                for q in range(NQ):
                    src = adj[bass.ds(v * SPAN + h * HALF, HALF), SPAN * k + QCOLS * q:SPAN * k + QCOLS * (q + 1)]
                    sp.dma_start(raw[R * q:R * (q + 1), slot, :].rearrange("p (g x) -> p g x", g=STRIPS),
                                 src.rearrange("(g s) x -> s g x", s=R)).then_inc(slot_in[slot], 16)

            def load_natural(e, v, slot):
                k, hh = divmod(e, 2)
                for q in (1, 2, 3, 0):
                    r0 = SPAN * k + QCOLS * q + P * hh
                    src = adj[r0:r0 + P, bass.ds(v * SPAN, SPAN)]
                    sp.dma_start(raw[R * q:R * (q + 1), slot, :].rearrange("p (j x) -> p j x", j=4),
                                 src.rearrange("(j r) x -> r j x", r=R)).then_inc(slot_in[slot], 16)

            def load_x(at, spans):
                load_x_spans(sp, at, spans)

            def pass0(v):
                for e in range(PIECES):
                    n = v * PIECES + e
                    if not isinstance(n, int) or n >= 2:
                        sp.wait_ge(unit_turned, (n - 1) * UPP)
                    load_turned(e, v, 2 * (e % 2))
                    if not isinstance(n, int) or n >= 2:
                        sp.wait_ge(natural_used, n - 1)
                        sp.wait_ge(row_summed, (n - 1) * 4)
                    load_natural(e, v, 2 * (e % 2) + 1)

            def store(v, g):
                sp.wait_ge(sum_ready, v * 2 + g + 1)
                for q in range(NQ):
                    sp.dma_start(out[bass.ds(v * SPAN + QCOLS * q + P * g, P), :].rearrange("(j r) d -> r j d", r=R),
                                 x2[R * q:R * (q + 1), bass.ds(v * NCX + 4 * g, 4), :]).then_inc(stored, 16)

            def later_pass(ps, v, stores):
                for e in range(PIECES):
                    if ps == 1 and isinstance(v, int) and v == 0 and e < SLOTS:
                        if e == 0:
                            sp.wait_ge(unit_turned, PASS_UNITS - UPP)
                        elif e == 1:
                            sp.wait_ge(natural_used, ITERS * PIECES - 1)
                            sp.wait_ge(row_summed, ITERS * C - 4)
                            load_x(1, range(C // NCX))
                            sp.wait_ge(unit_turned, PASS_UNITS)
                        elif e == 2:
                            sp.wait_ge(natural_used, ITERS * PIECES)
                            sp.wait_ge(row_summed, ITERS * C)
                        else:
                            sp.wait_ge(x_added, C)
                    else:
                        sp.wait_ge(unit_turned, ps * PASS_UNITS + v * UNITS + (e - 3) * UPP)
                    load_turned(e, v, SLOT_OF[e % SLOTS])
                    if stores and e == 6:
                        store(v - 1, 0)
                        store(v - 1, 1)

            load_x(0, (0, 1))
            for dst, src in ((w_in_sb, w_in), (w_out_sb, w_out), (w_sage_sb, w_sage)):
                sp.dma_start(dst[:, :], src).then_inc(w_loaded, 16)
            for j in range(4):
                sp.dma_start(bias_row[0:1, j, :], bias.rearrange("(a d) -> a d", a=1)).then_inc(w_loaded, 16)
            pass0(0)
            with sp.Fori(1, ITERS) as v:
                pass0(v)
            for ps in (1, 2):
                later_pass(ps, 0, False)
                with sp.Fori(1, ITERS) as v:
                    later_pass(ps, v, ps == 2)
            store(ITERS - 1, 0)
            store(ITERS - 1, 1)
            sp.wait_ge(stored, 2 * ITERS * LOAD)

        @block.vector
        def _(dve):
            steps = [0]

            def step(ins):
                steps[0] += 1
                ins.then_inc(dve_step, 1)

            def settle():
                dve.wait_ge(dve_step, steps[0])

            def turn(ps, v, u):
                unit = ps * PASS_UNITS + v * UNITS + u
                e, w = divmod(u, UPP)
                if ps == 0:
                    slot, loads = 2 * (e % 2), v * (PIECES // 2) + e // 2 + 1
                else:
                    slot = SLOT_OF[e % SLOTS]
                    loads = ITERS * PIECES // 2 + ((ps - 1) * ITERS + v) * (PIECES // SLOTS) + e // SLOTS + 1
                if w == 0:
                    dve.wait_ge(slot_in[slot], loads * LOAD)
                wait_unless_none(dve, unit_used, unit - TDEPTH + 1)
                src = raw[:, slot, :].rearrange("p (g x) -> p g x", g=STRIPS)[:, :, 64 * w:64 * (w + 1)]
                dst = turned[:, turned_slot(u), :, :].rearrange("p c (g s) -> p g c s", s=R)
                nc.vector.transpose(dst, src).then_inc(unit_turned, 1)

            def split_low(ps, v, u):
                unit = ps * PASS_UNITS + v * UNITS + u
                dve.wait_ge(high_ready, splits(ps, v, u) + 1)
                wait_unless_none(dve, unit_used, split_free(ps, unit))
                t = turned[:, turned_slot(u), :, :]
                if ps == 0:
                    nc.vector.tensor_tensor(low[:, 0:2, :], t, high[:, 0:2, :].bitcast(F32),
                                            ALU.subtract).then_inc(low_ready, 1)
                else:
                    nc.vector.tensor_tensor(low[:, u % 4, :], t[:, 1, :], high[:, u % 4, :].bitcast(F32),
                                            ALU.subtract).then_inc(low_ready, 1)

            def stage_half(v, h):
                dve.wait_ge(unit_used, v * UNITS + (h + 1) * (UNITS // 2))
                if h == 0:
                    wait_unless_none(dve, project_done, v * 4)
                nc.vector.tensor_copy(stage[:, 0, :, 2 * h:2 * h + 2, :].rearrange("p c q s -> p q c s"),
                                      half_sum[h][:, :].rearrange("p (q c s) -> p q c s", q=2, s=R)
                                      ).then_inc(half_staged, 1)

            def stage_panel(v):
                dve.wait_ge(natural_used, (v + 1) * PIECES)
                for h in range(2):
                    last = nc.vector.tensor_copy(stage[:, 1, :, 2 * h:2 * h + 2, :].rearrange("p c q s -> p q c s"),
                                                 panel_sum[h][:, :].rearrange("p (q c s) -> p q c s", q=2, s=R))
                    last.then_inc(panel_staged, 1)

            def keep_project(v, g):
                dve.wait_ge(project_done, v * 4 + g + 1)
                dst = (x2 if g < 2 else p2)[:, :, :].rearrange("p c d -> p (c d)")
                nc.vector.tensor_copy(dst[:, bass.ds(v * SPAN + (g % 2) * HALF, HALF)],
                                      project[g % 2][:, :]).then_inc(project_read, 1)

            def pass0(v, prev, hooks={}):
                for u in range(UNITS):
                    turn(0, *((v, u + 1) if u + 1 < UNITS else (v + 1, 0)))
                    if u % 2 == 0:
                        split_low(0, v, u)
                    if prev is not None and u == 2:
                        stage_half(prev, 1)
                        stage_panel(prev)
                    if prev is not None and u in (6, 8):
                        for g in (0, 1):
                            keep_project(prev, u - 6 + g)
                    if u == 17:
                        stage_half(v, 0)
                    if u in hooks:
                        hooks[u]()

            def norm_scale(src, call):
                g, side = call % ITERS, call % 2
                for j in range(NCX):
                    step(nc.vector.bn_stats(stats[:, j, :], src[:, NCX * g + j, :]))
                settle()
                for j in range(NCX):
                    step(nc.vector.bn_aggr(mean_var[:, j, :], stats[:, j, :]))
                settle()
                if call >= 2:
                    dve.wait_ge(h_written, call - 1)
                nc.vector.tensor_scalar(var[:, side, :], mean_var[:, :, 1], EPS, None, ALU.add).then_inc(var_ready, 1)
                dve.wait_ge(std_ready, call + 1)
                step(nc.vector.reciprocal(inv_std[:, side, :], std[:, side, :]))
                settle()
                if call not in DVE_NORMS:
                    nc.vector.scalar_tensor_tensor(out=shift[:, side, :], in0=mean_var[:, :, 0], scalar=-1.0,
                                                   in1=inv_std[:, side, :], op0=ALU.mult, op1=ALU.mult
                                                   ).then_inc(scale_ready, 1)
                    return
                if call == ITERS:
                    dve.wait_ge(unit_used, PASS_UNITS)
                    dve.wait_ge(natural_used, ITERS * PIECES)
                for j in range(NCX):
                    ins = nc.vector.tensor_scalar(h_full[:, NCX * g + j, :], src[:, NCX * g + j, :],
                                                  mean_var[:, j, 0:1], inv_std[:, side, j:j + 1],
                                                  ALU.subtract, ALU.mult)
                ins.then_inc(scale_ready, 1)
                dve.wait_ge(scale_ready, call + 1)

            def first_norm(g):
                dve.wait_ge(x_in[g], LOAD)
                norm_scale(x_rows[0], g)

            def second_norm(g):
                blocks = range(NCX * g, NCX * (g + 1))
                if g == 0:
                    dve.wait_ge(x_in[g], 2 * LOAD)
                    for c in blocks:
                        nc.vector.scalar_tensor_tensor(out=x2[:, c, :], in0=x2[:, c, :], scalar=inv_deg[:, 0, c:c + 1],
                                                       in1=x_rows[1][:, c, :], op0=ALU.mult, op1=ALU.add
                                                       ).then_inc(x_added, 1)
                dve.wait_ge(x_added, NCX * (g + 1))
                dve.wait_ge(project_read, 4 * (g + 1))
                for c in blocks:
                    step(nc.vector.scalar_tensor_tensor(out=x2[:, c, :], in0=p2[:, c, :], scalar=inv_deg[:, 1, c:c + 1],
                                                        in1=x2[:, c, :], op0=ALU.mult, op1=ALU.add))
                settle()
                norm_scale(x2, ITERS + g)

            nc.vector.memset(ones_row[:, :], 1.0).then_inc(ones_set, 1)
            first_norm(0)
            first_norm(1)
            turn(0, 0, 0)
            pass0(0, None, {1: lambda: first_norm(2), 4: lambda: first_norm(3)})
            with dve.Fori(1, ITERS) as v:
                pass0(v, v - 1)
            turn(1, 0, 1)

            dve.wait_ge(row_summed, ITERS * C)
            dve.wait_ge(high_ready, PASS_UNITS)
            step(nc.vector.tensor_reduce(deg[:, 0, :], row_part[:, :].rearrange("p (v c) -> p c v", c=C),
                                         AX.X, ALU.add))
            step(nc.vector.tensor_reduce(deg[:, 1, :], col_part[:, :].rearrange("p (v c) -> p c v", c=C),
                                         AX.X, ALU.add))
            settle()
            step(nc.vector.tensor_scalar(positive[:, :, :], deg[:, :, :], 0.0, None, ALU.is_gt))
            settle()
            step(nc.vector.tensor_tensor(deg[:, :, :], deg[:, :, :], positive[:, :, :], ALU.mult))
            settle()
            step(nc.vector.tensor_tensor(deg[:, :, :], deg[:, :, :], positive[:, :, :], ALU.subtract))
            settle()
            step(nc.vector.tensor_scalar(deg[:, :, :], deg[:, :, :], 1.0, None, ALU.add))
            settle()
            nc.vector.reciprocal(inv_deg[:, :, :], deg[:, :, :]).then_inc(deg_ready, 1)
            dve.wait_ge(deg_ready, 1)
            second_norm(0)
            turn(1, 0, 2)
            turn(1, 0, 3)
            second_norm(1)

            def keep_last(z):
                keep_project(ITERS - 1, 2 * z)
                keep_project(ITERS - 1, 2 * z + 1)

            def finish_y(v):
                for g in range(2):
                    dve.wait_ge(y_high_ready, v * 2 + g + 1)
                    nc.vector.tensor_tensor(y_low[:, bass.ds(v * 4 + 2 * g, 2), :],
                                            small[:, g, 0:2 * D].rearrange("p (c d) -> p c d", d=D),
                                            y_high[:, bass.ds(v * 4 + 2 * g, 2), :].bitcast(F32),
                                            ALU.subtract).then_inc(y_ready, 1)

            def finish_out(v):
                for g in range(2):
                    dve.wait_ge(swish_ready, v * 2 + g + 1)
                    place = x2[:, bass.ds(v * NCX + 4 * g, 4), :]
                    nc.vector.tensor_tensor(place, small[:, g, :].rearrange("p (c d) -> p c d", d=D), place,
                                            ALU.add).then_inc(sum_ready, 1)

            def later_pass(ps, v, finish, turned_before=1, hooks={}, last=False):
                for u in range(UNITS):
                    if u + 1 < UNITS:
                        if u + 1 >= turned_before:
                            turn(ps, v, u + 1)
                    elif not last:
                        turn(ps, v + 1, 0)
                    if u % 2 == 0 and not whole_unit(ps, v, u):
                        split_low(ps, v, u)
                    if finish is not None and u == 10:
                        finish()
                    if u in hooks:
                        hooks[u]()

            later_pass(1, 0, None, turned_before=4, hooks={
                3: lambda: keep_last(0), 4: lambda: second_norm(2), 5: lambda: keep_last(1),
                8: lambda: second_norm(3)})
            with dve.Fori(1, ITERS) as v:
                later_pass(1, v, lambda: finish_y(v - 1))
            later_pass(2, 0, lambda: finish_y(ITERS - 1))
            with dve.Fori(1, ITERS - 1) as v:
                later_pass(2, v, lambda: finish_out(v - 1))
            later_pass(2, ITERS - 1, lambda: finish_out(ITERS - 2), last=True)
            finish_out(ITERS - 1)

        @block.gpsimd
        def _(pool):
            def low_parts(ps, v, hooks={}):
                for u in range(1, UNITS, 2):
                    if u in hooks:
                        hooks[u]()
                    if whole_unit(ps, v, u):
                        continue
                    unit = ps * PASS_UNITS + v * UNITS + u
                    pool.wait_ge(high_ready, splits(ps, v, u) + 1)
                    wait_unless_none(pool, unit_used, split_free(ps, unit))
                    if ps == 0:
                        nc.gpsimd.tensor_tensor(low[:, 2:4, :], turned[:, turned_slot(u), :, :],
                                                high[:, 2:4, :].bitcast(F32), ALU.subtract).then_inc(pool_low_ready, 1)
                    else:
                        nc.gpsimd.tensor_tensor(low[:, u % 4, :], turned[:, turned_slot(u), 1, :],
                                                high[:, u % 4, :].bitcast(F32), ALU.subtract).then_inc(pool_low_ready, 1)

            def low_h(call):
                pool.wait_ge(h_high_ready, call + 1)
                group = slice(NCX * (call % ITERS), NCX * (call % ITERS + 1))
                nc.gpsimd.tensor_tensor(h_low[:, group, :], h_full[:, group, :], h_high[:, group, :].bitcast(F32),
                                        ALU.subtract).then_inc(h_ready, 1)

            def add_x(g):
                pool.wait_ge(x_in[g], 2 * LOAD)
                if g == ITERS - 1:
                    pool.wait_ge(project_read, 4 * ITERS - 2)
                for c in range(NCX * g, NCX * (g + 1)):
                    nc.gpsimd.tensor_scalar(x2[:, c, :], x2[:, c, :], inv_deg[:, 0, c:c + 1], 0.0,
                                            ALU.mult, ALU.add).then_inc(x_scaled, 1)
                pool.wait_ge(x_scaled, NCX * g)
                group = slice(NCX * g, NCX * (g + 1))
                nc.gpsimd.tensor_tensor(x2[:, group, :], x2[:, group, :], x_rows[1][:, group, :],
                                        ALU.add).then_inc(x_added, NCX)

            low_h(0)
            low_h(1)
            low_parts(0, 0, {3: lambda: low_h(2), 7: lambda: low_h(3)})
            with pool.Fori(1, ITERS) as v:
                low_parts(0, v)
            pool.wait_ge(deg_ready, 1)
            for g in range(1, ITERS):
                pool.wait_ge(x_added, NCX)
                add_x(g)
                if g >= 2:
                    low_h(ITERS + g - 2)
            low_h(2 * ITERS - 2)
            low_h(2 * ITERS - 1)
            for ps in (1, 2):
                low_parts(ps, 0)
                with pool.Fori(1, ITERS) as v:
                    low_parts(ps, v)

        @block.scalar
        def _(act):
            def split_high(ps, v, u):
                if whole_unit(ps, v, u):
                    return
                unit = ps * PASS_UNITS + v * UNITS + u
                act.wait_ge(unit_turned, unit + 1)
                wait_unless_none(act, unit_used, split_free(ps, unit))
                t = turned[:, turned_slot(u), :, :]
                if ps == 0:
                    h, c = divmod(2 * u, C)
                    for j in range(2):
                        ins = nc.scalar.activation(
                            high[:, 2 * (u % 2) + j, :], t[:, j, :], ACT.Copy,
                            accum_out=col_part[:, bass.ds(v * 2 * C + h * C + c + j, 1)])
                    ins.then_inc(high_ready, 1)
                else:
                    nc.scalar.activation(high[:, u % 4, :], t[:, 1, :], ACT.Copy).then_inc(high_ready, 1)

            def sum_rows(v, b):
                e, j = divmod(b, 4)
                slot = 2 * (e % 2) + 1
                if j == 0:
                    act.wait_ge(slot_in[slot], (v * (PIECES // 2) + e // 2 + 1) * LOAD)
                wait_unless_none(act, row_summed, v * C + b)
                nc.scalar.activation(discard, raw[:, slot, SPAN * j:SPAN * (j + 1)], ACT.Copy,
                                     accum_out=row_part[:, bass.ds(v * C + b, 1)]).then_inc(row_summed, 1)

            def write_h(call):
                g, side = call % ITERS, call % 2
                src = x_rows[0] if call < ITERS else x2
                act.wait_ge(var_ready, call + 1)
                nc.scalar.activation(std[:, side, :], var[:, side, :], ACT.Sqrt).then_inc(std_ready, 1)
                act.wait_ge(scale_ready, call + 1)
                group = slice(NCX * g, NCX * (g + 1))
                if call in DVE_NORMS:
                    nc.scalar.activation(h_full[:, group, :], h_full[:, group, :], ACT.Relu).then_inc(h_written, 1)
                else:
                    for j in range(NCX):
                        c = NCX * g + j
                        ins = nc.scalar.activation(h_full[:, c, :], src[:, c, :], ACT.Relu,
                                                   bias=shift[:, side, j:j + 1], scale=inv_std[:, side, j:j + 1])
                    ins.then_inc(h_written, 1)
                act.wait_ge(h_written, call + 1)
                nc.scalar.activation(h_high[:, group, :], h_full[:, group, :], ACT.Copy).then_inc(h_high_ready, 1)

            load_x_spans(act, 0, (2, 3))
            write_h(0)
            write_h(1)

            def pass0(v, hooks={}):
                for u in range(UNITS):
                    split_high(0, v, u)
                    if u in hooks:
                        hooks[u]()
                    sum_rows(v, u)

            pass0(0, {1: lambda: write_h(2), 4: lambda: write_h(3)})
            with act.Fori(1, ITERS) as v:
                pass0(v)
            write_h(ITERS)
            act.wait_ge(project_done, 4 * (ITERS - 1))
            act.wait_ge(unit_used, PASS_UNITS)
            nc.scalar.activation(stage[:, 0, :, 2:4, :].rearrange("p c q s -> p q c s"),
                                 half_sum[1][:, :].rearrange("p (q c s) -> p q c s", q=2, s=R),
                                 ACT.Copy).then_inc(half_staged, 1)
            act.wait_ge(natural_used, ITERS * PIECES)
            for h in range(2):
                nc.scalar.activation(stage[:, 1, :, 2 * h:2 * h + 2, :].rearrange("p c q s -> p q c s"),
                                     panel_sum[h][:, :].rearrange("p (q c s) -> p q c s", q=2, s=R),
                                     ACT.Copy).then_inc(panel_staged, 1)
            for call in range(ITERS + 1, 2 * ITERS):
                write_h(call)

            def stage_half(ps, v, h):
                act.wait_ge(unit_used, (ps * ITERS + v) * UNITS + (h + 1) * (UNITS // 2))
                act.wait_ge(project_done, 4 * ITERS + ((ps - 1) * ITERS + v) * 2)
                nc.scalar.activation(late_stage[:, :, 2 * h:2 * h + 2, :].rearrange("p c q s -> p q c s"),
                                     half_sum[h][:, :].rearrange("p (q c s) -> p q c s", q=2, s=R),
                                     ACT.Copy).then_inc(half_staged, 1)

            def swish_y(v):
                for g in range(2):
                    act.wait_ge(project_done, 4 * ITERS + v * 2 + g + 1)
                    z = project[g][:, :].rearrange("p (b two d) -> p b two d", two=2, d=D)
                    nc.scalar.activation(y_full[:, bass.ds(v * 4 + 2 * g, 2), :], z[:, :, 0, :], ACT.Silu)
                    nc.scalar.activation(small[:, g, 0:2 * D].rearrange("p (c d) -> p c d", d=D), z[:, :, 1, :],
                                         ACT.Silu)
                    nc.scalar.activation(y_high[:, bass.ds(v * 4 + 2 * g, 2), :], z[:, :, 1, :],
                                         ACT.Silu).then_inc(y_high_ready, 1)

            def swish_out(v):
                for g in range(2):
                    act.wait_ge(project_done, 6 * ITERS + v * 2 + g + 1)
                    act.wait_ge(y_ready, 2 * ITERS)
                    nc.scalar.activation(small[:, g, :], project[g][:, :], ACT.Silu).then_inc(swish_ready, 1)

            def later_pass(ps, v, prev, swish):
                for u in range(UNITS):
                    split_high(ps, v, u)
                    if prev is not None and u == 3:
                        stage_half(prev[0], prev[1], 1)
                    if prev is not None and u == 8:
                        swish()
                    if u == 19:
                        stage_half(ps, v, 0)

            later_pass(1, 0, None, None)
            with act.Fori(1, ITERS) as v:
                later_pass(1, v, (1, v - 1), lambda: swish_y(v - 1))
            later_pass(2, 0, (1, ITERS - 1), lambda: swish_y(ITERS - 1))
            with act.Fori(1, ITERS) as v:
                later_pass(2, v, (2, v - 1), lambda: swish_out(v - 1))
            stage_half(2, ITERS - 1, 1)
            swish_out(ITERS - 1)

        @block.tensor
        def _(pe):
            def turned_unit(ps, v, u):
                unit = ps * PASS_UNITS + v * UNITS + u
                h, c = divmod(2 * u, C)
                if u % (UNITS // 2) == 0:
                    wait_unless_none(pe, half_staged, (ps * ITERS + v) * 2 + h - 1)
                acc = half_sum[h][:, :]
                if whole_unit(ps, v, u):
                    pe.wait_ge(unit_turned, unit + 1)
                    for j in range(2):
                        ins = nc.tensor.matmul(acc, h_full[:, c + j, :], turned[:, turned_slot(u), j, :],
                                               start=c + j == 0, stop=c + j == C - 1)
                    return ins
                pe.wait_ge(high_ready, splits(ps, v, u) + 1)
                pe.wait_ge((low_ready, pool_low_ready)[u % 2], splits_of_kind(ps, v, u) + 1)
                if ps > 0:
                    whole = h_full[:, c, :] if ps == 1 else y_full[:, c // 2, :]
                    nc.tensor.matmul(acc, whole, turned[:, turned_slot(u), 0, :], start=c == 0, stop=False)
                for j in range(2) if ps == 0 else (1,):
                    s = 2 * (u % 2) + j if ps == 0 else u % 4
                    if ps < 2:
                        hh, hl = h_high[:, c + j, :], h_low[:, c + j, :]
                    else:
                        hh, hl = y_high[:, c // 2, :], y_low[:, c // 2, :]
                    nc.tensor.matmul(acc, hh, high[:, s, :], start=ps == 0 and c + j == 0, stop=False)
                    nc.tensor.matmul(acc, hh, low[:, s, :], start=False, stop=False)
                    ins = nc.tensor.matmul(acc, hl, high[:, s, :], start=False, stop=c + j == C - 1)
                return ins

            def natural(v, b):
                e, j = divmod(b, 4)
                slot = 2 * (e % 2) + 1
                if j == 0:
                    pe.wait_ge(slot_in[slot], (v * (PIECES // 2) + e // 2 + 1) * LOAD)
                if b == 0:
                    wait_unless_none(pe, panel_staged, v * 2)
                for hh in range(2):
                    a = raw[:, slot, SPAN * j + HALF * hh:SPAN * j + HALF * (hh + 1)]
                    ins = nc.tensor.matmul(panel_sum[hh][:, :], h_full[:, b, :], a, start=b == 0, stop=b == C - 1)
                if j == 3:
                    ins.then_inc(natural_used, 1)

            def weights0(v, z):
                pe.wait_ge(half_staged, v * 2 + 2)
                pe.wait_ge(panel_staged, v * 2 + 2)
                for g in range(2):
                    if z == 1:
                        pe.wait_ge(project_read, v * 4 + g + 1)
                    for j in range(4):
                        ins = nc.tensor.matmul(project[g][:, D * j:D * (j + 1)],
                                               stage[:, z, 4 * g + j, :, :].rearrange("p q s -> p (q s)"),
                                               (w_in_sb if z == 0 else w_out_sb)[:, :], start=True, stop=True)
                    ins.then_inc(project_done, 1)

            def later_weights(ps, v):
                pe.wait_ge(half_staged, (ps * ITERS + v) * 2 + 2)
                for g in range(2):
                    pe.wait_ge(*((project_read, 4 * ITERS) if ps == 1 else (y_high_ready, 2 * ITERS)))
                    nc.tensor.matmul(project[g][:, :], ones_row[:, :], bias_row[:, :, :].rearrange("p j d -> p (j d)"),
                                     start=True, stop=False)
                    for j in range(4):
                        ins = nc.tensor.matmul(project[g][:, D * j:D * (j + 1)],
                                               late_stage[:, 4 * g + j, :, :].rearrange("p q s -> p (q s)"),
                                               w_sage_sb[:, :], start=False, stop=j == 3)
                    ins.then_inc(project_done, 1)

            def pass0(v, prev):
                for u in range(UNITS):
                    if u < UNITS // 2 and isinstance(v, int) and u % 4 == 0:
                        pe.wait_ge(h_ready, u // 4 + 1)
                    ins = turned_unit(0, v, u)
                    ins.then_inc(unit_used, 1)
                    for b in natural_blocks(u):
                        natural(v, b)
                    if prev is not None and u in (3, 5):
                        weights0(prev, (u - 3) // 2)

            pe.wait_ge(w_loaded, 7 * 16)
            pe.wait_ge(ones_set, 1)
            pass0(0, None)
            with pe.Fori(1, ITERS) as v:
                pass0(v, v - 1)

            def later_pass(ps, v, prev):
                for u in range(UNITS):
                    if whole_unit(ps, v, u) and u % 4 == 0:
                        pe.wait_ge(h_written, ITERS + u // 4 + 1)
                    if isinstance(v, int) and ps == 1 and v == 0 and u == WHOLE:
                        pe.wait_ge(h_ready, 2 * ITERS)
                    if isinstance(v, int) and ps == 2 and v == 0 and u < UNITS // 2 and u % 4 == 0:
                        pe.wait_ge(y_ready, 2 * (u // 4 + 1))
                    ins = turned_unit(ps, v, u)
                    ins.then_inc(unit_used, 1)
                    if prev is not None and u == 4:
                        later_weights(*prev)
                    if isinstance(v, int) and ps == 1 and v == 0 and u in (1, 3):
                        weights0(ITERS - 1, u // 2)

            later_pass(1, 0, None)
            with pe.Fori(1, ITERS) as v:
                later_pass(1, v, (1, v - 1))
            later_pass(2, 0, (1, ITERS - 1))
            with pe.Fori(1, ITERS) as v:
                later_pass(2, v, (2, v - 1))
            later_weights(2, ITERS - 1)


_INS = ["x", "adj", "L0_gnn_W_in", "L0_gnn_W_out", "L1_gnn_W", "L1_gnn_b"]


def kernel(**inputs):
    import numpy as _np
    import concourse.bacc as _bacc
    from concourse import mybir as _mybir
    from concourse.bass_utils import run_bass_kernel_spmd as _run

    nc = _bacc.Bacc("TRN2", target_bir_lowering=False, num_devices=1)
    arrays, args = {}, []
    for name in _INS:
        a = _np.ascontiguousarray(inputs[name])
        arrays[f"in_{name}_dram"] = a
        args.append(nc.dram_tensor(f"in_{name}_dram", a.shape, _mybir.dt.from_np(a.dtype), kind="ExternalInput").ap())
    args.append(nc.dram_tensor("out_0_dram", (4096, 128), _mybir.dt.float32, kind="ExternalOutput").ap())
    gnn_kernel(nc, *args)
    r = _run(nc, [arrays], core_ids=[0])
    return r.results[0]["out_0_dram"]
```

```python
from contextlib import ExitStack

import concourse.bass as bass
from concourse import mybir

F32, F32R = mybir.dt.float32, mybir.dt.float32r
ACT = mybir.ActivationFunctionType
ALU = mybir.AluOpType
AX = mybir.AxisListType

N = 4096
D = 128
P = 128
NQ, R = 4, 32
SPAN = 1024
HALF = 512
ITERS = N // SPAN
NCX = SPAN // P
C = N // P
STRIPS = HALF // R
QCOLS = SPAN // NQ
PIECES = 2 * C // NCX
UPP = 4
UNITS = PIECES * UPP
PASS_UNITS = ITERS * UNITS
SLOTS = 4
TDEPTH = 4
ORDER = ((0, 1, 2, 3), (2, 3, 1, 0), (2, 0, 1, 3))
SLOT_OF = ((0, 2, 0, 2), (0, 2, 3, 1), (0, 1, 3, 2))
SPLIT_OF = ((1,), (1,), (1,), (0, 1))
RING_OF = (0, 1, 2, 3)
RING = sum(len(s) for s in SPLIT_OF)
SPLIT_CX = tuple(2 * w + j for w in range(UPP) for j in SPLIT_OF[w])
WHOLE_CX = tuple(cx for cx in range(NCX) if cx not in SPLIT_CX)
LEAD = 2
DVE_NORMS = (0,)
WHOLE = UNITS // 2
LOAD = 16 * NQ
EPS = 1e-5


def y_place(b):
    k, cx = divmod(b, NCX)
    return len(SPLIT_CX) * k + SPLIT_CX.index(cx) if cx in SPLIT_CX else len(WHOLE_CX) * k + WHOLE_CX.index(cx)


def rows_of(ps, v):
    return v if ps == 1 else v * -1 + (ITERS - 1)


def half_of(ps, p):
    return 1 - p if ps == 1 else p


def block_at(ps, c):
    return NCX * ORDER[ps][c // NCX] + c % NCX


def blocks_after(u):
    return (u - 1,) * (u > 0) + (u,) * (u == UNITS - 1)


def gnn_kernel(nc, x, adj, w_in, w_out, w_sage, bias, out):
    ctx = ExitStack()
    with ctx:
        def sb(name, shape, dt=F32):
            return ctx.enter_context(nc.sbuf_tensor(name, shape, dt))

        def bank(name):
            return ctx.enter_context(nc.psum_tensor(name, [P, HALF], F32))

        def sem(name):
            return ctx.enter_context(nc.semaphore(name))

        raw = sb("raw", [P, SLOTS, STRIPS * QCOLS])
        turned = sb("turned", [P, TDEPTH, 2, HALF])
        high = sb("high", [P, RING, HALF], F32R)
        low = sb("low", [P, RING, HALF], F32R)
        h_full = sb("h_full", [P, C, D])
        h_high = sb("h_high", [P, C, D], F32R)
        h_low = sb("h_low", [P, C, D], F32R)
        y_high = sb("y_high", [P, C // NCX * len(SPLIT_CX), D], F32R)
        y_low = sb("y_low", [P, C // NCX * len(SPLIT_CX), D], F32R)
        x2 = sb("x2", [P, C, D])
        p2 = sb("p2", [P, C, D])
        w_in_sb = sb("w_in_sb", [P, D])
        w_out_sb = sb("w_out_sb", [P, D])
        w_sage_sb = sb("w_sage_sb", [P, D])
        bias_low = sb("bias_low", [1, D], F32R)
        bias_parts = sb("bias_parts", [2, 4, D], F32R)
        ones = sb("ones", [2, P], F32R)
        row_part = sb("row_part", [P, ITERS * C])
        col_part = sb("col_part", [P, 2 * ITERS * C])
        stats = sb("stats", [P, NCX, 6])
        mean_var = sb("mean_var", [P, NCX, 2])
        var = sb("var", [P, 2, NCX])
        std = sb("std", [P, 2, NCX])
        inv_std = sb("inv_std", [P, 2, NCX])
        shift = sb("shift", [P, 2, NCX])
        deg = sb("deg", [P, 2, C])
        not_positive = sb("not_positive", [P, 2, C])
        inv_deg = sb("inv_deg", [P, 2, C])

        stage = h_full[:, 0:2 * NCX, :].rearrange("p (z c q) (t s) -> p z c (q t) s", z=2, c=NCX, t=4)
        nat_high = y_high[:, 0:2 * NCX, :].rearrange("p (two c) d -> p two (c d)", two=2)
        nat_low = y_low[:, 0:2 * NCX, :].rearrange("p (two c) d -> p two (c d)", two=2)
        x_rows = [x2, raw[:, 1, :].rearrange("p (c d) -> p c d", d=D)]
        small = p2[:, :, :].rearrange("p (z b) d -> p z (b d)", b=4)
        y_full = p2[:, C // 2:C, :]
        bias_row = p2[0:1, 0:4, :]
        late_stage = small[:, 2:4, :].rearrange("p z x -> p (z x)").rearrange(
            "p (c q s) -> p c q s", c=NCX, q=NQ)

        half_sum = [bank("half_sum0"), bank("half_sum1")]
        panel_sum = [bank("panel_sum0"), bank("panel_sum1")]
        project = [bank("project0"), bank("project1")]

        x_in = [sem(f"x_in{k}") for k in range(C // NCX)]
        w_loaded = sem("w_loaded")
        ones_set = sem("ones_set")
        bias_high_ready = sem("bias_high_ready")
        bias_low_ready = sem("bias_low_ready")
        bias_ready = sem("bias_ready")
        natural_in = [sem(f"natural_in{i}") for i in range(SLOTS)]
        nat_low_ready = sem("nat_low_ready")
        pool_nat_low_ready = sem("pool_nat_low_ready")
        slot_in = [sem(f"slot_in{i}") for i in range(SLOTS)]
        unit_turned = sem("unit_turned")
        high_ready = sem("high_ready")
        low_ready = sem("low_ready")
        pool_low_ready = sem("pool_low_ready")
        unit_used = sem("unit_used")
        natural_used = sem("natural_used")
        row_summed = sem("row_summed")
        half_staged = sem("half_staged")
        panel_staged = sem("panel_staged")
        project_done = sem("project_done")
        project_read = sem("project_read")
        dve_step = sem("dve_step")
        var_ready = sem("var_ready")
        std_ready = sem("std_ready")
        scale_ready = sem("scale_ready")
        h_written = sem("h_written")
        h2_begun = sem("h2_begun")
        deg_ready = sem("deg_ready")
        x_added = sem("x_added")
        x_scaled = sem("x_scaled")
        p2_scaled = sem("p2_scaled")
        x2_ready = sem("x2_ready")
        h_high_ready = sem("h_high_ready")
        h_ready = sem("h_ready")
        y_high_ready = sem("y_high_ready")
        y_ready = sem("y_ready")
        swish_ready = sem("swish_ready")
        sum_ready = sem("sum_ready")
        stored = sem("stored")

        block = ctx.enter_context(nc.Block())

        def turned_slot(unit):
            return unit % TDEPTH

        def span_of(call):
            return ORDER[call // ITERS][call % ITERS]

        def loads_before(ps, v, e):
            if ps == 0:
                return v * (PIECES // 2) + e // 2
            return (ITERS * PIECES // 2 * (SLOT_OF[ps][e % SLOTS] % 2 == 0)
                    + ((ps - 1) * ITERS + v) * (PIECES // SLOTS) + e // SLOTS)

        def y_group(v, g):
            before = sum(cx < 4 * g for cx in SPLIT_CX)
            return v * len(SPLIT_CX) + before, sum(4 * g <= cx < 4 * g + 4 for cx in SPLIT_CX)

        def natural_block(b):
            return raw[:, 2 * (b // 4 % 2) + 1, SPAN * (b % 4):SPAN * (b % 4 + 1)]

        def split_free(ps, unit):
            return unit - 1 if ps == 0 else unit - UPP + 1

        def splits(ps, v, u):
            before = ps * PASS_UNITS + v * UNITS + u
            return before if ps == 0 else before - WHOLE

        def by_pool(ps, u):
            return u % 2 == 1 if ps == 0 else u % UPP > 0

        def lows_before(ps, v, u):
            if ps == 0:
                return v * (UNITS // 2) + u // 2
            pieces = ((ps - 1) * ITERS + v) * PIECES + u // UPP - WHOLE // UPP
            return PASS_UNITS // 2 + (pieces * (UPP - 1) + u % UPP - 1 if by_pool(ps, u) else pieces)

        def split_views(ps, u):
            if ps == 0:
                return slice(0, 2), slice(2 * (u % 2), 2 * (u % 2) + 2)
            w = u % UPP
            return slice(SPLIT_OF[w][0], 2), slice(RING_OF[w], RING_OF[w] + len(SPLIT_OF[w]))

        def whole_unit(ps, v, u):
            return ps == 1 and isinstance(v, int) and v == 0 and u < WHOLE

        def wait_unless_none(eng, sem_, value):
            if not isinstance(value, int) or value > 0:
                eng.wait_ge(sem_, value)

        def store_blocks(eng, v, g):
            eng.wait_ge(sum_ready, v * 2 + g + 1)
            k = rows_of(2, v)
            for q in range(NQ):
                eng.dma_start(out[bass.ds(k * SPAN + QCOLS * q + P * g, P), :].rearrange("(j r) d -> r j d", r=R),
                              x2[R * q:R * (q + 1), bass.ds(k * NCX + 4 * g, 4), :]).then_inc(stored, 16)

        @block.sync
        def _(sp):
            def load_turned(ps, e, v):
                h, k, slot = half_of(ps, e // SLOTS), ORDER[ps][e % SLOTS], SLOT_OF[ps][e % SLOTS]
                for q in (1, 2, 3, 0):
                    c0 = SPAN * k + QCOLS * q
                    src = adj[bass.ds(rows_of(ps, v) * SPAN + h * HALF, HALF), c0:c0 + QCOLS]
                    sp.dma_start(raw[R * q:R * (q + 1), slot, :].rearrange("p (g x) -> p g x", g=STRIPS),
                                 src.rearrange("(g s) x -> s g x", s=R)).then_inc(slot_in[slot], 16)

            def load_natural(i, v):
                e, part = divmod(i, 2)
                k, hh = divmod(e, 2)
                dst = raw[:, 2 * (e % 2) + 1, 2 * SPAN * part:2 * SPAN * (part + 1)]
                for q in (1, 2, 3, 0):
                    r0 = SPAN * k + QCOLS * q + P * hh + 2 * R * part
                    src = adj[r0:r0 + 2 * R, bass.ds(rows_of(0, v) * SPAN, SPAN)]
                    sp.dma_start(dst[R * q:R * (q + 1), :].rearrange("p (j x) -> p j x", j=2),
                                 src.rearrange("(j r) x -> r j x", r=R)).then_inc(natural_in[i % SLOTS], 16)

            def load_x(at, spans):
                for k in spans:
                    for q in range(NQ):
                        r0 = SPAN * k + QCOLS * q
                        sp.dma_start(x_rows[at][R * q:R * (q + 1), NCX * k:NCX * (k + 1), :],
                                      x[r0:r0 + QCOLS, :].rearrange("(c r) d -> r c d", r=R)).then_inc(x_in[k], 16)

            def pass0(v, first=None):
                for e in range(PIECES):
                    n = v * PIECES + e
                    if not isinstance(n, int) or n >= 2:
                        sp.wait_ge(unit_turned, (n - 1) * UPP)
                    load_turned(0, e, v)
                    for i in (2 * e, 2 * e + 1):
                        if first is not None and e == 0:
                            load_x(0, (2 + i,))
                        wait_unless_none(sp, natural_used, v * C + 2 * i - 6)
                        load_natural(i, v)
                    if first is not None and e == 0:
                        first()
                    if first is not None and e == 6:
                        move_bias_low()

            def move_bias_low():
                sp.wait_ge(bias_low_ready, 1)
                for j in range(4):
                    sp.dma_start(bias_parts[1:2, j, :].bitcast(F32), bias_low[:, :].bitcast(F32)).then_inc(bias_ready, 16)

            def later_pass(ps, v, stores):
                for e in range(PIECES):
                    first = isinstance(v, int) and e < SLOTS
                    if first and (ps == 2 or e < 2):
                        slot = SLOT_OF[ps][e]
                        sp.wait_ge(slot_in[slot], LOAD * loads_before(ps, 0, e))
                        sp.sem_inc(slot_in[slot], LOAD)
                        continue
                    if first and e == 2:
                        sp.wait_ge(natural_used, ITERS * C - 4)
                        load_x(1, ORDER[1])
                        sp.wait_ge(natural_used, ITERS * C)
                    elif first:
                        sp.wait_ge(x_added, C)
                    else:
                        sp.wait_ge(unit_turned, ps * PASS_UNITS + v * UNITS + (e - 3) * UPP)
                    load_turned(ps, e, v)
                    if stores and e == 6:
                        store_blocks(sp, v - 1, 0)
                        store_blocks(sp, v - 1, 1)

            def load_weights():
                for dst, src in ((w_in_sb, w_in), (w_out_sb, w_out), (w_sage_sb, w_sage)):
                    sp.dma_start(dst[:, :], src).then_inc(w_loaded, 16)
                for j in range(4):
                    sp.dma_start(bias_row[:, j, :], bias.rearrange("(a d) -> a d", a=1)).then_inc(w_loaded, 16)

            load_x(0, (0, 1))
            pass0(0, load_weights)
            with sp.Fori(1, ITERS) as v:
                pass0(v)
            for ps in (1, 2):
                later_pass(ps, 0, False)
                with sp.Fori(1, ITERS) as v:
                    later_pass(ps, v, ps == 2)
            store_blocks(sp, ITERS - 1, 0)
            sp.wait_ge(stored, 2 * ITERS * LOAD)

        @block.vector
        def _(dve):
            steps = [0]

            def step(ins):
                steps[0] += 1
                ins.then_inc(dve_step, 1)

            def settle():
                dve.wait_ge(dve_step, steps[0])

            def turn(ps, v, u):
                unit = ps * PASS_UNITS + v * UNITS + u
                e, w = divmod(u, UPP)
                slot = SLOT_OF[ps][e % SLOTS]
                if w == 0:
                    dve.wait_ge(slot_in[slot], (loads_before(ps, v, e) + 1) * LOAD)
                wait_unless_none(dve, unit_used, unit - TDEPTH + 1)
                src = raw[:, slot, :].rearrange("p (g x) -> p g x", g=STRIPS)[:, :, 64 * w:64 * (w + 1)]
                dst = turned[:, turned_slot(u), :, :].rearrange("p c (g s) -> p g c s", s=R)
                nc.vector.transpose(dst, src).then_inc(unit_turned, 1)

            def split_low(ps, v, u):
                unit = ps * PASS_UNITS + v * UNITS + u
                dve.wait_ge(high_ready, splits(ps, v, u) + 1)
                wait_unless_none(dve, unit_used, split_free(ps, unit))
                blocks, places = split_views(ps, u)
                nc.vector.tensor_tensor(low[:, places, :], turned[:, turned_slot(u), blocks, :],
                                        high[:, places, :].bitcast(F32), ALU.subtract).then_inc(low_ready, 1)

            def stage_half(v, h):
                dve.wait_ge(unit_used, v * UNITS + (h + 1) * (UNITS // 2))
                if h == 0:
                    wait_unless_none(dve, project_done, v * 4)
                nc.vector.tensor_copy(stage[:, 0, :, 2 * h:2 * h + 2, :].rearrange("p c q s -> p q c s"),
                                      half_sum[h][:, :].rearrange("p (q c s) -> p q c s", q=2, s=R)
                                      ).then_inc(half_staged, 1)

            def keep_project(v, g):
                dve.wait_ge(project_done, v * 4 + g + 1)
                dst = (x2 if g < 2 else p2)[:, :, :].rearrange("p c d -> p (c d)")
                nc.vector.tensor_copy(dst[:, bass.ds(rows_of(0, v) * SPAN + (g % 2) * HALF, HALF)],
                                      project[g % 2][:, :]).then_inc(project_read, 1)

            def split_natural(v, b):
                dve.wait_ge(row_summed, v * C + b + 1)
                nc.vector.tensor_tensor(nat_low[:, b % 2, :], natural_block(b), nat_high[:, b % 2, :].bitcast(F32),
                                        ALU.subtract).then_inc(nat_low_ready, 1)

            def turn_ahead(ps, v, u):
                turn(ps, *((v, u) if u < UNITS else (v + 1, u - UNITS)))

            def pass0(v, prev, hooks={}):
                for u in range(UNITS):
                    if prev is None and u < UPP:
                        turn_ahead(0, v, u + LEAD)
                    if u % 2 == 0:
                        split_low(0, v, u)
                    else:
                        split_natural(v, u - 1)
                    if prev is not None or u >= UPP:
                        turn_ahead(0, v, u + LEAD)
                    if prev is not None and u == 6:
                        stage_half(prev, 1)
                    if prev is not None and u in (12, 13, 16, 17):
                        keep_project(prev, {12: 0, 13: 1, 16: 2, 17: 3}[u])
                    if u == 20:
                        stage_half(v, 0)
                    if u in hooks:
                        hooks[u]()

            def moments(src, call):
                g, side = span_of(call), call % 2
                for j in range(NCX):
                    step(nc.vector.bn_stats(stats[:, j, :], src[:, NCX * g + j, :]))
                settle()
                for j in range(NCX):
                    step(nc.vector.bn_aggr(mean_var[:, j, :], stats[:, j, :]))
                settle()
                if call >= 2:
                    dve.wait_ge(h_written, call - 1)
                nc.vector.tensor_scalar(var[:, side, :], mean_var[:, :, 1], EPS, None, ALU.add).then_inc(var_ready, 1)

            def norm_scale(src, call):
                g, side = span_of(call), call % 2
                dve.wait_ge(std_ready, call + 1)
                step(nc.vector.reciprocal(inv_std[:, side, :], std[:, side, :]))
                settle()
                if call not in DVE_NORMS:
                    nc.vector.scalar_tensor_tensor(out=shift[:, side, :], in0=mean_var[:, :, 0], scalar=-1.0,
                                                   in1=inv_std[:, side, :], op0=ALU.mult, op1=ALU.mult
                                                   ).then_inc(scale_ready, 1)
                    return
                for j in range(NCX):
                    ins = nc.vector.tensor_scalar(h_full[:, NCX * g + j, :], src[:, NCX * g + j, :],
                                                  mean_var[:, j, 0:1], inv_std[:, side, j:j + 1],
                                                  ALU.subtract, ALU.mult)
                ins.then_inc(scale_ready, 1)
                dve.wait_ge(scale_ready, call + 1)

            def first_moments(g):
                dve.wait_ge(x_in[g], LOAD)
                moments(x_rows[0], g)

            def second_norm(i):
                g = span_of(ITERS + i)
                blocks = range(NCX * g, NCX * (g + 1))
                if i == 0:
                    dve.wait_ge(x_in[g], 2 * LOAD)
                    for c in blocks:
                        nc.vector.scalar_tensor_tensor(out=x2[:, c, :], in0=x2[:, c, :], scalar=inv_deg[:, 0, c:c + 1],
                                                       in1=x_rows[1][:, c, :], op0=ALU.mult, op1=ALU.add
                                                       ).then_inc(x_added, 1)
                if i < 2:
                    dve.wait_ge(x_added, NCX * (i + 1))
                    for c in blocks:
                        step(nc.vector.scalar_tensor_tensor(out=x2[:, c, :], in0=p2[:, c, :],
                                                            scalar=inv_deg[:, 1, c:c + 1], in1=x2[:, c, :],
                                                            op0=ALU.mult, op1=ALU.add))
                    settle()
                else:
                    dve.wait_ge(x2_ready, i - 1)
                moments(x2, ITERS + i)
                norm_scale(x2, ITERS + i)

            def split_bias():
                dve.wait_ge(bias_high_ready, 1)
                nc.vector.tensor_tensor(bias_low[:, :], bias_row[:, 0, :], bias_parts[0:1, 0, :].bitcast(F32),
                                        ALU.subtract).then_inc(bias_low_ready, 1)

            nc.vector.memset(ones[:, :].bitcast(F32), 1.0).then_inc(ones_set, 1)
            first_moments(0)
            norm_scale(x_rows[0], 0)
            first_moments(1)
            turn(0, 0, 0)
            turn(0, 0, 1)
            norm_scale(x_rows[0], 1)
            first_moments(2)

            def next_norm():
                norm_scale(x_rows[0], 2)
                first_moments(3)

            def low_h(call):
                dve.wait_ge(h_ready, call)
                dve.wait_ge(h_high_ready, call + 1)
                group = slice(NCX * span_of(call), NCX * (span_of(call) + 1))
                nc.vector.tensor_tensor(h_low[:, group, :], h_full[:, group, :], h_high[:, group, :].bitcast(F32),
                                        ALU.subtract).then_inc(h_ready, 1)

            pass0(0, None, {0: next_norm, 2: lambda: norm_scale(x_rows[0], 3), 4: lambda: low_h(2),
                            8: lambda: low_h(3), 12: split_bias})
            with dve.Fori(1, ITERS) as v:
                pass0(v, v - 1)
            dve.wait_ge(row_summed, ITERS * C)
            dve.wait_ge(high_ready, PASS_UNITS)
            step(nc.vector.tensor_reduce(deg[:, 0, :], row_part[:, :].rearrange("p (v c) -> p c v", c=C),
                                         AX.X, ALU.add))
            step(nc.vector.tensor_reduce(deg[:, 1, :], col_part[:, :].rearrange("p (v c) -> p c v", c=C),
                                         AX.X, ALU.add))
            settle()
            step(nc.vector.tensor_scalar(not_positive[:, :, :], deg[:, :, :], 0.0, None, ALU.is_le))
            settle()
            step(nc.vector.scalar_tensor_tensor(out=deg[:, :, :], in0=deg[:, :, :], scalar=0.0, in1=not_positive[:, :, :],
                                                op0=ALU.max, op1=ALU.add))
            settle()
            nc.vector.reciprocal(inv_deg[:, :, :], deg[:, :, :]).then_inc(deg_ready, 1)
            dve.wait_ge(deg_ready, 1)
            second_norm(0)
            turn(1, 0, 2)
            turn(1, 0, 3)
            second_norm(1)

            def finish_y(v):
                for g in range(2):
                    dve.wait_ge(y_high_ready, v * 2 + g + 1)
                    place, n = y_group(v, g)
                    nc.vector.tensor_tensor(y_low[:, bass.ds(place, n), :],
                                            small[:, g, 0:n * D].rearrange("p (c d) -> p c d", d=D),
                                            y_high[:, bass.ds(place, n), :].bitcast(F32),
                                            ALU.subtract).then_inc(y_ready, 1)

            def finish_out(v):
                for g in range(2):
                    dve.wait_ge(swish_ready, v * 2 + g + 1)
                    place = x2[:, bass.ds(rows_of(2, v) * NCX + 4 * g, 4), :]
                    nc.vector.tensor_tensor(place, small[:, g, :].rearrange("p (c d) -> p c d", d=D), place,
                                            ALU.add).then_inc(sum_ready, 1)

            def later_pass(ps, v, finish, turned_before=LEAD, hooks={}, last=False):
                for u in range(UNITS):
                    if not by_pool(ps, u) and not whole_unit(ps, v, u):
                        split_low(ps, v, u)
                    if u + LEAD >= turned_before and not (last and u + LEAD >= UNITS):
                        turn_ahead(ps, v, u + LEAD)
                    if finish is not None and u == 10:
                        finish()
                    if u in hooks:
                        hooks[u]()

            later_pass(1, 0, None, turned_before=4, hooks={4: lambda: second_norm(2), 8: lambda: second_norm(3)})
            with dve.Fori(1, ITERS) as v:
                later_pass(1, v, lambda: finish_y(v - 1))
            later_pass(2, 0, lambda: finish_y(ITERS - 1))
            with dve.Fori(1, ITERS - 1) as v:
                later_pass(2, v, lambda: finish_out(v - 1))
            later_pass(2, ITERS - 1, lambda: finish_out(ITERS - 2), last=True)
            finish_out(ITERS - 1)

        @block.gpsimd
        def _(pool):
            def low_parts(ps, v, hooks={}):
                for u in range(UNITS):
                    if u in hooks:
                        hooks[u]()
                    if not by_pool(ps, u) or whole_unit(ps, v, u):
                        continue
                    unit = ps * PASS_UNITS + v * UNITS + u
                    pool.wait_ge(high_ready, splits(ps, v, u) + 1)
                    wait_unless_none(pool, unit_used, split_free(ps, unit))
                    blocks, places = split_views(ps, u)
                    nc.gpsimd.tensor_tensor(low[:, places, :], turned[:, turned_slot(u), blocks, :],
                                            high[:, places, :].bitcast(F32), ALU.subtract).then_inc(pool_low_ready, 1)
                    if ps == 0:
                        pool.wait_ge(row_summed, v * C + u + 1)
                        nc.gpsimd.tensor_tensor(nat_low[:, u % 2, :], natural_block(u),
                                                nat_high[:, u % 2, :].bitcast(F32),
                                                ALU.subtract).then_inc(pool_nat_low_ready, 1)

            def low_h(call):
                pool.wait_ge(h_high_ready, call + 1)
                group = slice(NCX * span_of(call), NCX * (span_of(call) + 1))
                nc.gpsimd.tensor_tensor(h_low[:, group, :], h_full[:, group, :], h_high[:, group, :].bitcast(F32),
                                        ALU.subtract).then_inc(h_ready, 1)

            def add_x(i):
                g = span_of(ITERS + i)
                pool.wait_ge(x_in[g], 2 * LOAD)
                if g == rows_of(0, ITERS - 1):
                    pool.wait_ge(project_read, 4 * ITERS - 2)
                for c in range(NCX * g, NCX * (g + 1)):
                    nc.gpsimd.tensor_scalar(x2[:, c, :], x2[:, c, :], inv_deg[:, 0, c:c + 1], 0.0,
                                            ALU.mult, ALU.add).then_inc(x_scaled, 1)
                pool.wait_ge(x_scaled, NCX * i)
                group = slice(NCX * g, NCX * (g + 1))
                nc.gpsimd.tensor_tensor(x2[:, group, :], x2[:, group, :], x_rows[1][:, group, :],
                                        ALU.add).then_inc(x_added, NCX)
                if i == 1:
                    return
                pool.wait_ge(x_added, NCX * (i + 1))
                pool.wait_ge(p2_scaled, i - 1)
                nc.gpsimd.tensor_tensor(x2[:, group, :], x2[:, group, :], p2[:, group, :], ALU.add).then_inc(x2_ready, 1)

            low_h(0)
            low_parts(0, 0, {3: lambda: low_h(1)})
            with pool.Fori(1, ITERS) as v:
                low_parts(0, v)
            pool.wait_ge(deg_ready, 1)
            pool.wait_ge(x_added, NCX)
            for i in range(1, ITERS):
                add_x(i)
                if i >= 2:
                    low_h(ITERS + i - 2)
            low_h(2 * ITERS - 2)
            low_h(2 * ITERS - 1)
            for ps in (1, 2):
                low_parts(ps, 0)
                with pool.Fori(1, ITERS) as v:
                    low_parts(ps, v)

        @block.scalar
        def _(act):
            def split_high(ps, v, u):
                if whole_unit(ps, v, u):
                    return
                unit = ps * PASS_UNITS + v * UNITS + u
                act.wait_ge(unit_turned, unit + 1)
                wait_unless_none(act, unit_used, split_free(ps, unit))
                t = turned[:, turned_slot(u), :, :]
                if ps == 0:
                    h, c = divmod(2 * u, C)
                    for j in range(2):
                        ins = nc.scalar.activation(
                            high[:, 2 * (u % 2) + j, :], t[:, j, :], ACT.Copy,
                            accum_out=col_part[:, bass.ds(v * 2 * C + h * C + c + j, 1)])
                    ins.then_inc(high_ready, 1)
                else:
                    blocks, places = split_views(ps, u)
                    nc.scalar.activation(high[:, places, :], t[:, blocks, :], ACT.Copy).then_inc(high_ready, 1)

            def sum_rows(v, b):
                if b % 2 == 0:
                    act.wait_ge(natural_in[b // 2 % SLOTS], (v * (C // 2 // SLOTS) + b // 8 + 1) * LOAD)
                wait_unless_none(act, natural_used, v * C + b - 1)
                nc.scalar.activation(nat_high[:, b % 2, :], natural_block(b), ACT.Copy,
                                     accum_out=row_part[:, bass.ds(v * C + b, 1)]).then_inc(row_summed, 1)

            def stage_panel(v):
                act.wait_ge(natural_used, (v + 1) * C)
                for h in range(2):
                    nc.scalar.activation(stage[:, 1, :, 2 * h:2 * h + 2, :].rearrange("p c q s -> p q c s"),
                                         panel_sum[h][:, :].rearrange("p (q c s) -> p q c s", q=2, s=R),
                                         ACT.Copy).then_inc(panel_staged, 1)

            def take_root(call):
                act.wait_ge(var_ready, call + 1)
                nc.scalar.activation(std[:, call % 2, :], var[:, call % 2, :], ACT.Sqrt).then_inc(std_ready, 1)

            def write_h(call):
                g, side = span_of(call), call % 2
                src = x_rows[0] if call < ITERS else x2
                act.wait_ge(scale_ready, call + 1)
                group = slice(NCX * g, NCX * (g + 1))
                if call in DVE_NORMS:
                    nc.scalar.activation(h_full[:, group, :], h_full[:, group, :], ACT.Relu).then_inc(h_written, 1)
                else:
                    for j in range(NCX):
                        c = NCX * g + j
                        ins = nc.scalar.activation(h_full[:, c, :], src[:, c, :], ACT.Relu,
                                                   bias=shift[:, side, j:j + 1], scale=inv_std[:, side, j:j + 1])
                        if call >= ITERS and j < NCX - 1:
                            ins.then_inc(h2_begun, 1)
                    ins.then_inc(h_written, 1)
                act.wait_ge(h_written, call + 1)
                nc.scalar.activation(h_high[:, group, :], h_full[:, group, :], ACT.Copy).then_inc(h_high_ready, 1)

            def pass0(v, prev, hooks={}):
                for u in range(UNITS):
                    split_high(0, v, u)
                    if prev is not None and u == 1:
                        stage_panel(prev)
                    for b in blocks_after(u):
                        sum_rows(v, b)
                    if u in hooks:
                        hooks[u]()

            def split_bias():
                act.wait_ge(w_loaded, 7 * 16)
                nc.scalar.activation(bias_parts[0:1, :, :], bias_row[:, :, :], ACT.Copy).then_inc(bias_high_ready, 1)

            def next_h(call):
                write_h(call)
                take_root(call + 1)

            take_root(0)
            next_h(0)
            pass0(0, None, {0: lambda: next_h(1), 1: lambda: next_h(2), 3: lambda: write_h(3), 12: split_bias})
            with act.Fori(1, ITERS) as v:
                pass0(v, v - 1)
            act.wait_ge(project_done, 4 * (ITERS - 1))
            act.wait_ge(unit_used, PASS_UNITS)
            nc.scalar.activation(stage[:, 0, :, 2:4, :].rearrange("p c q s -> p q c s"),
                                 half_sum[1][:, :].rearrange("p (q c s) -> p q c s", q=2, s=R),
                                 ACT.Copy).then_inc(half_staged, 1)
            stage_panel(ITERS - 1)

            def keep_last(z):
                for g in range(2):
                    act.wait_ge(project_done, 4 * (ITERS - 1) + 2 * z + g + 1)
                    dst = (x2, p2)[z][:, :, :].rearrange("p c d -> p (c d)")
                    first = rows_of(0, ITERS - 1) * SPAN + g * HALF
                    nc.scalar.activation(dst[:, first:first + HALF], project[g][:, :], ACT.Copy).then_inc(project_read, 1)

            def scale_p2(i):
                g = span_of(ITERS + i)
                if i == 2:
                    act.wait_ge(deg_ready, 1)
                if g == rows_of(0, ITERS - 1):
                    act.wait_ge(project_read, 4 * ITERS)
                for c in range(NCX * g, NCX * (g + 1)):
                    ins = nc.scalar.activation(p2[:, c, :], p2[:, c, :], ACT.Copy, scale=inv_deg[:, 1, c:c + 1])
                ins.then_inc(p2_scaled, 1)

            keep_last(0)
            scale_p2(2)
            take_root(ITERS)
            write_h(ITERS)
            keep_last(1)
            take_root(ITERS + 1)
            write_h(ITERS + 1)
            scale_p2(3)
            for call in (ITERS + 2, ITERS + 3):
                take_root(call)
                write_h(call)

            def stage_half(ps, v, p):
                h = half_of(ps, p)
                act.wait_ge(unit_used, (ps * ITERS + v) * UNITS + (p + 1) * (UNITS // 2))
                act.wait_ge(project_done, 4 * ITERS + ((ps - 1) * ITERS + v) * 2)
                nc.scalar.activation(late_stage[:, :, 2 * h:2 * h + 2, :].rearrange("p c q s -> p q c s"),
                                     half_sum[p][:, :].rearrange("p (q c s) -> p q c s", q=2, s=R),
                                     ACT.Copy).then_inc(half_staged, 1)

            def swish_y(v):
                for g in range(2):
                    act.wait_ge(project_done, 4 * ITERS + v * 2 + g + 1)
                    z = project[g][:, :].rearrange("p (c d) -> p c d", d=D)
                    if g == 0:
                        z = project[g][:, :].rearrange("p (b two d) -> p two b d", two=2, d=D)
                        whole, split = z[:, 0, :, :], z[:, 1, :, :]
                    else:
                        whole, split = z[:, 0:1, :], z[:, 1:4, :]
                    place, n = y_group(v, g)
                    nc.scalar.activation(y_full[:, bass.ds(v * len(WHOLE_CX) + 2 * g, 4 - n), :], whole, ACT.Silu)
                    nc.scalar.activation(small[:, g, 0:n * D].rearrange("p (c d) -> p c d", d=D), split, ACT.Silu)
                    nc.scalar.activation(y_high[:, bass.ds(place, n), :], split, ACT.Silu).then_inc(y_high_ready, 1)

            def swish_out(v):
                for g in range(2):
                    act.wait_ge(project_done, 6 * ITERS + v * 2 + g + 1)
                    act.wait_ge(y_ready, 2 * ITERS)
                    nc.scalar.activation(small[:, g, :], project[g][:, :], ACT.Silu).then_inc(swish_ready, 1)

            def later_pass(ps, v, prev, swish):
                for u in range(UNITS):
                    split_high(ps, v, u)
                    if prev is not None and u == 3:
                        stage_half(prev[0], prev[1], 1)
                    if prev is not None and u == 8:
                        swish()
                    if u == 19:
                        stage_half(ps, v, 0)

            later_pass(1, 0, None, None)
            with act.Fori(1, ITERS) as v:
                later_pass(1, v, (1, v - 1), lambda: swish_y(v - 1))
            later_pass(2, 0, (1, ITERS - 1), lambda: swish_y(ITERS - 1))
            with act.Fori(1, ITERS) as v:
                later_pass(2, v, (2, v - 1), lambda: swish_out(v - 1))
            stage_half(2, ITERS - 1, 1)
            swish_out(ITERS - 1)
            store_blocks(act, ITERS - 1, 1)

        @block.tensor
        def _(pe):
            def turned_unit(ps, v, u):
                unit = ps * PASS_UNITS + v * UNITS + u
                h, c = divmod(2 * u, C)
                if u % (UNITS // 2) == 0:
                    wait_unless_none(pe, half_staged, (ps * ITERS + v) * 2 + h - 1)
                acc = half_sum[h][:, :]
                blocks = [block_at(ps, c), block_at(ps, c + 1)]
                if whole_unit(ps, v, u):
                    pe.wait_ge(unit_turned, unit + 1)
                    for j in range(2):
                        ins = nc.tensor.matmul(acc, h_full[:, blocks[j], :], turned[:, turned_slot(u), j, :],
                                               start=c + j == 0, stop=c + j == C - 1)
                    return ins
                pe.wait_ge(high_ready, splits(ps, v, u) + 1)
                first = 2 * (u % 2) if ps == 0 else RING_OF[u % UPP]
                split = (0, 1) if ps == 0 else SPLIT_OF[u % UPP]
                if ps < 2:
                    parts = [(h_high[:, blocks[j], :], h_low[:, blocks[j], :], first + i) for i, j in enumerate(split)]
                else:
                    parts = [(y_high[:, y_place(blocks[j]), :], y_low[:, y_place(blocks[j]), :], first + i)
                             for i, j in enumerate(split)]
                if 0 not in split:
                    whole = h_full[:, blocks[0], :] if ps == 1 else y_full[:, y_place(blocks[0]), :]
                    nc.tensor.matmul(acc, whole, turned[:, turned_slot(u), 0, :], start=c == 0, stop=False)
                for hh, hl, s in parts:
                    nc.tensor.matmul(acc, hh, high[:, s, :], start=ps == 0 and c == 0 and s == first, stop=False)
                    nc.tensor.matmul(acc, hl, high[:, s, :], start=False, stop=False)
                pe.wait_ge(pool_low_ready if by_pool(ps, u) else low_ready, lows_before(ps, v, u) + 1)
                for hh, hl, s in parts:
                    ins = nc.tensor.matmul(acc, hh, low[:, s, :], start=False,
                                           stop=c == C - 2 and s == parts[-1][2])
                return ins

            def natural(v, b):
                if b == 0:
                    wait_unless_none(pe, panel_staged, v * 2)
                halves = [(panel_sum[hh][:, :], slice(HALF * hh, HALF * (hh + 1))) for hh in range(2)]
                pe.wait_ge(row_summed, v * C + b + 1)
                for acc, half in halves:
                    nc.tensor.matmul(acc, h_high[:, b, :], nat_high[:, b % 2, half], start=b == 0, stop=False)
                for acc, half in halves:
                    nc.tensor.matmul(acc, h_low[:, b, :], nat_high[:, b % 2, half], start=False, stop=False)
                pe.wait_ge((nat_low_ready, pool_nat_low_ready)[b % 2], v * (C // 2) + b // 2 + 1)
                for acc, half in halves:
                    ins = nc.tensor.matmul(acc, h_high[:, b, :], nat_low[:, b % 2, half], start=False, stop=b == C - 1)
                ins.then_inc(natural_used, 1)

            def weights0(v, z):
                pe.wait_ge(*((half_staged, v * 2 + 2) if z == 0 else (panel_staged, v * 2 + 2)))
                for g in range(2):
                    if z == 1:
                        pe.wait_ge(project_read, v * 4 + g + 1)
                    for j in range(4):
                        ins = nc.tensor.matmul(project[g][:, D * j:D * (j + 1)],
                                               stage[:, z, 4 * g + j, :, :].rearrange("p q s -> p (q s)"),
                                               (w_in_sb if z == 0 else w_out_sb)[:, :], start=True, stop=True)
                    ins.then_inc(project_done, 1)

            def later_weights(ps, v):
                pe.wait_ge(half_staged, (ps * ITERS + v) * 2 + 2)
                for g in range(2):
                    pe.wait_ge(*((project_read, 4 * ITERS) if ps == 1 else (y_high_ready, 2 * ITERS)))
                    nc.tensor.matmul(project[g][:, :], ones[:, :], bias_parts[:, :, :].rearrange("p j d -> p (j d)"),
                                     start=True, stop=False)
                    for j in range(4):
                        ins = nc.tensor.matmul(project[g][:, D * j:D * (j + 1)],
                                               late_stage[:, 4 * g + j, :, :].rearrange("p q s -> p (q s)"),
                                               w_sage_sb[:, :], start=False, stop=j == 3)
                    ins.then_inc(project_done, 1)

            def pass0(v, prev):
                for u in range(UNITS):
                    if u < UNITS // 2 and isinstance(v, int) and u % 4 == 0:
                        pe.wait_ge(h_ready, u // 4 + 1)
                    ins = turned_unit(0, v, u)
                    ins.then_inc(unit_used, 1)
                    for b in blocks_after(u):
                        natural(v, b)
                    if prev is not None and u in (9, 13):
                        weights0(prev, (u - 9) // 4)

            pass0(0, None)
            pe.wait_ge(w_loaded, 7 * 16)
            pe.wait_ge(ones_set, 1)
            pe.wait_ge(bias_ready, 4 * 16)
            with pe.Fori(1, ITERS) as v:
                pass0(v, v - 1)

            def later_pass(ps, v, prev):
                for u in range(UNITS):
                    if whole_unit(ps, v, u):
                        i, w = divmod(u, UPP)
                        if w < UPP - 1:
                            pe.wait_ge(h2_begun, (NCX - 1) * i + 2 * w + 2)
                        else:
                            pe.wait_ge(h_written, ITERS + i + 1)
                    if isinstance(v, int) and ps == 1 and v == 0 and u == WHOLE:
                        pe.wait_ge(h_ready, 2 * ITERS)
                    if isinstance(v, int) and ps == 2 and v == 0 and u < UNITS // 2 and u % 4 == 0:
                        pe.wait_ge(y_ready, 2 * (max(ORDER[2][:u // 4 + 1]) + 1))
                    ins = turned_unit(ps, v, u)
                    ins.then_inc(unit_used, 1)
                    if prev is not None and u == 4:
                        later_weights(*prev)

            weights0(ITERS - 1, 0)
            weights0(ITERS - 1, 1)
            later_pass(1, 0, None)
            with pe.Fori(1, ITERS) as v:
                later_pass(1, v, (1, v - 1))
            later_pass(2, 0, (1, ITERS - 1))
            with pe.Fori(1, ITERS) as v:
                later_pass(2, v, (2, v - 1))
            later_weights(2, ITERS - 1)


_INS = ["x", "adj", "L0_gnn_W_in", "L0_gnn_W_out", "L1_gnn_W", "L1_gnn_b"]


def kernel(**inputs):
    import numpy as _np
    import concourse.bacc as _bacc
    from concourse import mybir as _mybir
    from concourse.bass_utils import run_bass_kernel_spmd as _run

    nc = _bacc.Bacc("TRN2", target_bir_lowering=False, num_devices=1)
    arrays, args = {}, []
    for name in _INS:
        a = _np.ascontiguousarray(inputs[name])
        arrays[f"in_{name}_dram"] = a
        args.append(nc.dram_tensor(f"in_{name}_dram", a.shape, _mybir.dt.from_np(a.dtype), kind="ExternalInput").ap())
    args.append(nc.dram_tensor("out_0_dram", (4096, 128), _mybir.dt.float32, kind="ExternalOutput").ap())
    gnn_kernel(nc, *args)
    r = _run(nc, [arrays], core_ids=[0])
    return r.results[0]["out_0_dram"]
```
